# Optimizing a Trainium2 kernel written in Bass

```python
import numpy as np
import jax
import jax.numpy as jnp

def _softmax(x, axis=-1):
    return jax.nn.softmax(x, axis=axis)

def _gelu(x):
    return jax.nn.gelu(x, approximate=True)

def _silu(x):
    return jax.nn.silu(x)

def _sigmoid(x):
    return jax.nn.sigmoid(x)

def _layernorm(x, axis=-1, eps=1e-05):
    m = jnp.mean(x, axis=axis, keepdims=True)
    v = jnp.var(x, axis=axis, keepdims=True)
    return (x - m) / jnp.sqrt(v + eps)

def _scatter_add(tgt, idx, src, axis=0):
    return tgt.at[idx].add(src)

def _segment_sum(src, seg, n):
    return jax.ops.segment_sum(src, seg, n)
kernel_name = 'mk_adj_resnorm_d1_adj_r2_c253b2'

def setup_inputs(seed: int=0):
    np.random.seed(seed)
    _w = jnp.asarray

    def _rec_inputs():
        import jax
        import jax.numpy as jnp
        _gk = jax.random.key(seed)
        x = -0.0005207 + 1.001 * jax.random.normal(jax.random.fold_in(_gk, 1), (8192, 128), jnp.float32)
        _w = (1.0 + jnp.arange(8192, dtype=jnp.float32)) ** (-0.5)
        _w = _w / _w.mean()
        _pij = jnp.clip(0.00195312 * _w[:, None] * _w[None, :], 0.0, 1.0)
        _a = jax.random.uniform(jax.random.fold_in(_gk, 2), (8192, 8192)) < _pij
        adj = _a.astype(jnp.int32)
        return (x, adj)
    x, adj = _rec_inputs()

    def _L0_gnn_setup():
        import jax, jax.numpy as jnp
        import numpy as np
        ALPHA = 0.2
        MASK_VAL = -9000000000000000.0
        key = jax.random.key(seed)
        k1, k2, k3, k4 = jax.random.split(key, 4)
        N, Fin, Fout = (4096, 128, 128)
        h = jax.random.normal(k1, (N, Fin), dtype=jnp.float32)
        adj = jax.random.randint(k2, (N, N), 0, 2, dtype=jnp.int32)
        W = jax.random.normal(k3, (Fin, Fout), dtype=jnp.float32) * 0.06
        a = jax.random.normal(k4, (2 * Fout, 1), dtype=jnp.float32) * 0.06
        return {'h': h, 'adj': adj, 'W': W, 'a': a}
    _L0_gnn_all = _L0_gnn_setup()
    _L0_gnn_in = {k: v for k, v in _L0_gnn_all.items() if k in ('W', 'a')}
    del _L0_gnn_all
    return {'x': x, 'adj': adj, 'L0_gnn_W': _L0_gnn_in['W'], 'L0_gnn_a': _L0_gnn_in['a']}

def reference(x, adj, L0_gnn_W, L0_gnn_a):
    import jax
    import jax.numpy as jnp

    def _L0_gnn_ref(h, adj, W, a):
        import jax, jax.numpy as jnp
        import numpy as np
        ALPHA = 0.2
        MASK_VAL = -9000000000000000.0
        Fout = W.shape[1]
        Wh = h @ W
        a1, a2 = (a[:Fout, 0], a[Fout:, 0])
        e = (Wh @ a1)[:, None] + (Wh @ a2)[None, :]
        e = jnp.where(e > 0, e, ALPHA * e)
        e = jnp.where(adj > 0, e, MASK_VAL)
        attention = jax.nn.softmax(e, axis=1)
        h_prime = attention @ Wh
        return jax.nn.elu(h_prime)
    x = _layernorm(x + _L0_gnn_ref(x, adj, L0_gnn_W, L0_gnn_a), axis=-1)
    return x

_drawn_inputs = setup_inputs


def setup_inputs(seed=0):
    import zlib

    import numpy as np

    out = dict(_drawn_inputs(seed))
    spreads = {}
    factors = {}
    for name, (base, spread) in spreads.items():
        noise = np.random.default_rng([zlib.crc32(name.encode()), seed]).standard_normal(out[name].shape)
        drawn = base * np.exp(spread * noise) if base else spread * noise
        out[name] = jnp.asarray(drawn.astype(out[name].dtype))
    for name, factor in factors.items():
        out[name] = (out[name] * factor).astype(out[name].dtype)
    return out
```

```python
from contextlib import ExitStack

import concourse.bass as bass
from concourse import mybir

ALU = mybir.AluOpType
ACT = mybir.ActivationFunctionType
F32 = mybir.dt.float32
F16 = mybir.dt.float16
I32 = mybir.dt.int32
AX = mybir.AxisListType
RMAX = bass.bass_isa.ReduceOp.max

P = 128
LEAK = 0.2
LN_EPS = 1e-5
TINY = 1e-30
V_TOP = 16384.0
EDGE_GAIN = 100.0



def gat_kernel(nc, x, adj, W, a, out):
    N, D = x.shape
    assert D == P and N % 512 == 0
    RB = 4
    GROUP = RB * P
    NG = N // GROUP
    NC = N // P
    CPU_ = 2
    UNITS = NC // CPU_
    SLAB_C = 4
    RING = 4
    BODY = RING * SLAB_C // CPU_
    NBODY = UNITS // BODY
    EB = 4
    C1 = D + 1
    CW = D + 2
    SLAB_U = SLAB_C // CPU_
    OCT = 4
    NOCT = NC // OCT

    with ExitStack() as ctx:
        def sb(name, shape, dt):
            return ctx.enter_context(nc.sbuf_tensor(name, shape, dt))

        def ps(name, shape, dt):
            return ctx.enter_context(nc.psum_tensor(name, shape, dt))

        def sem(name):
            return ctx.enter_context(nc.semaphore(name))

        slab = [sb(f"slab{k}", [P, RB, SLAB_C * P], I32) for k in range(RING)]
        V = sb("V", [P, NC, 4, C1], F16)
        s_row = sb("s_row", [P, N], F32)
        neg_t = sb("neg_t", [P, NC], F32)
        alpha = sb("alpha", [P, NC], F32)
        beta = sb("beta", [P, NC], F32)
        ident = sb("ident", [P, P], F32)
        edge_bias = sb("edge_bias", [P, 1], F32)
        wh_max = sb("wh_max", [P, 1], F32)
        mean_wh = sb("mean_wh", [P, D], F32)
        shared = sb("shared", [P, NC * CW], F32)
        wh = shared[:, :].rearrange("p (c w) -> p c w", w=CW)
        UW = CPU_ * GROUP
        halves = shared[:, :].bitcast(F16)
        edge = [halves[:, (3 * k) * UW:(3 * k + 1) * UW] for k in range(EB)]
        pos = [halves[:, (3 * k + 1) * UW:(3 * k + 2) * UW] for k in range(EB)]
        neg = [halves[:, (3 * k + 2) * UW:(3 * k + 3) * UW] for k in range(EB)]
        w_in = sb("w_in", [P, CW], F32)
        w_t = sb("w_t", [P, D], F32)
        a_in = sb("a_in", [P, 2], F32)
        ones = sb("ones", [P, P], F32)
        wa1 = sb("wa1", [P, P], F32)
        x_nat = [sb(f"x_nat{k}", [P, RB, D], F32) for k in range(2)]
        x_t = [sb(f"x_t{k}", [P, GROUP], F32) for k in range(2)]
        q1 = sb("q1", [P, NC], F32)
        q2 = sb("q2", [P, NC], F32)
        z08 = sb("z08", [P, NC], F32)
        zmin = sb("zmin", [P, NC], F32)
        zmax = sb("zmax", [P, NC], F32)
        stat = sb("stat", [P, 16], F32)
        gmax = sb("gmax", [P, NG], F32)
        v32 = [sb(f"v32_{k}", [P, OCT, C1], F32) for k in range(2)]
        x_res = sb("x_res", [P, RB, D], F32)
        low_part = sb("low_part", [P, RB, C1], F32)
        mix = sb("mix", [P, RB, C1], F32)
        empty = sb("empty", [P, RB], F32)
        den = sb("den", [P, RB], F32)
        rden = sb("rden", [P, RB], F32)
        rscale = sb("rscale", [P, RB], F32)
        fill = sb("fill", [P, RB, D], F32)
        h = sb("h", [P, RB, D], F32)
        hneg = sb("hneg", [P, RB, D], F32)
        hpos = sb("hpos", [P, RB, D], F32)
        bn = sb("bn", [P, RB, 6], F32)
        mv = sb("mv", [P, RB, 2], F32)
        numbers = sb("numbers", [P, 4], F32)
        veps = sb("veps", [P, RB], F32)
        rstd = sb("rstd", [P, RB], F32)
        y_out = sb("y_out", [P, RB, D], F32)

        psT = [ps(f"psT{k}", [P, CPU_ * GROUP], F32) for k in range(2)]
        acc = [ps(f"acc{r}", [P, 512], F32) for r in range(RB)]
        p_xt = [psT[k][:, 0:GROUP] for k in range(2)]
        p_srow = [psT[k][:, GROUP:2 * GROUP] for k in range(2)]
        p_wh = [[acc[2 * k][:, 0:2 * CW], acc[2 * k + 1][:, 0:2 * CW]] for k in range(2)]

        w_in_landed = sem("w_in_landed")
        x_landed = [sem(f"x_landed{k}") for k in range(2)]
        slab_landed = [sem(f"slab_landed{k}") for k in range(RING)]
        x_res_landed = sem("x_res_landed")
        out_stored = sem("out_stored")
        consts_ready = sem("consts_ready")
        wt_ready = sem("wt_ready")
        wt_copied = sem("wt_copied")
        xt_ready = sem("xt_ready")
        xt_copied = sem("xt_copied")
        wh_ready = sem("wh_ready")
        wh_copied = sem("wh_copied")
        srow_copied = sem("srow_copied")
        dve_step = sem("dve_step")
        pmax_in = sem("pmax_in")
        pmax_out = sem("pmax_out")
        z_ready = sem("z_ready")
        q_ready = sem("q_ready")
        qs_ready = sem("qs_ready")
        v32_ready = sem("v32_ready")
        v_high = sem("v_high")
        v_low = sem("v_low")
        psT_ready = sem("psT_ready")
        edge_ready = sem("edge_ready")
        pos_ready = sem("pos_ready")
        neg_ready = sem("neg_ready")
        unit_used = sem("unit_used")
        low_ready = sem("low_ready")
        mix_ready = sem("mix_ready")
        den_ready = sem("den_ready")
        inverse_ready = sem("inverse_ready")
        h_ready = sem("h_ready")
        elu_parts = sem("elu_parts")
        res_ready = sem("res_ready")
        bn_done = sem("bn_done")
        mv_ready = sem("mv_ready")
        y_ready = sem("y_ready")
        pool_step = sem("pool_step")

        x_groups = x.rearrange("(g r p) d -> g p r d", r=RB, p=P)
        out_groups = out.rearrange("(g r p) d -> g p r d", r=RB, p=P)
        adj_rows = adj.rearrange("(r p) m -> p r m", p=P)
        x_rows = x.rearrange("(r p) d -> p r d", p=P)
        out_rows = out.rearrange("(r p) d -> p r d", p=P)

        block = ctx.enter_context(nc.Block())

        @block.sync
        def _(sp):
            sp.dma_start(w_in[:, 0:D], W).then_inc(w_in_landed, 16)
            sp.dma_start(a_in[:, :], a.rearrange("(k p) o -> p (k o)", p=P),
                         allow_slow_non_contiguous=True).then_inc(w_in_landed, 16)
            for g in range(NG):
                if g >= 2:
                    sp.wait_ge(xt_ready, g - 1)
                sp.dma_start(x_nat[g % 2][:, :, :], x_groups[g]).then_inc(x_landed[g % 2], 16)

            def load_slab(g, s, k, n, first):
                if not first:
                    sp.wait_ge(psT_ready, SLAB_U * (n - RING + 1))
                sp.dma_start(slab[k][:, :, :],
                             adj_rows[:, bass.ds(g * RB, RB), bass.ds(s * (SLAB_C * P), SLAB_C * P)]
                             ).then_inc(slab_landed[k], 16)

            per_group = NC // SLAB_C
            for k in range(RING):
                load_slab(0, k, k, k, True)
            with sp.Fori(1, NBODY) as b:
                for k in range(RING):
                    load_slab(0, b * RING + k, k, b * RING + k, False)
            with sp.Fori(1, NG) as g:
                with sp.Fori(0, NBODY) as b:
                    for k in range(RING):
                        load_slab(g, b * RING + k, k, g * per_group + b * RING + k, False)
            sp.wait_ge(out_stored, 16 * NG)

        @block.gpsimd
        def _(pool):
            nc.gpsimd.memset(ones[:, :], 1.0).then_inc(pool_step, 1)
            nc.gpsimd.memset(ident[:, :], 0.0).then_inc(pool_step, 1)
            pool.wait_ge(pool_step, 2)
            nc.gpsimd.affine_select(out=ident[:, :], in_=ident[:, :], compare_op=ALU.not_equal, fill=1.0,
                                    base=0, pattern=[[-1, P]], channel_multiplier=1).then_inc(consts_ready, 1)
            nc.gpsimd.memset(edge_bias[:, :], -EDGE_GAIN / 2).then_inc(consts_ready, 1)
            for k, value in enumerate((0.0, -1.0, LN_EPS, -0.5)):
                ins = nc.gpsimd.memset(numbers[:, k:k + 1], value)
            ins.then_inc(consts_ready, 1)
            pool.wait_ge(pmax_in, 1)
            nc.gpsimd.partition_all_reduce(stat[:, 2:4], stat[:, 0:2], P, RMAX).then_inc(pmax_out, 1)

            def rows(m):
                return m.unsqueeze(2).broadcast_to([P, RB, D])

            def number(k, shape):
                ap = numbers[:, k:k + 1]
                return ap.unsqueeze(2).broadcast_to(shape) if len(shape) == 3 else ap.broadcast_to(shape)

            tt = nc.gpsimd.tensor_tensor
            full, few = [P, RB, D], [P, RB]
            STEPS = 7

            def epilogue(g):
                base = 2 + g * STEPS
                n = [0]

                def chain(ins):
                    ins.then_inc(pool_step, 1)
                    n[0] += 1
                    pool.wait_ge(pool_step, base + n[0])

                pool.wait_ge(inverse_ready, 2 * g + 2)
                chain(tt(fill[:, :, :], mean_wh[:, :].unsqueeze(1).broadcast_to(full), rows(empty[:, :]), ALU.mult))
                chain(tt(fill[:, :, :], fill[:, :, :], mix[:, :, 0:D], ALU.add))
                chain(tt(rscale[:, :], rden[:, :], wh_max[:, 0:1].broadcast_to(few), ALU.mult))
                tt(h[:, :, :], fill[:, :, :], rows(rscale[:, :]), ALU.mult).then_inc(h_ready, 1)
                pool.wait_ge(elu_parts, 3 * g + 3)
                chain(tt(h[:, :, :], hneg[:, :, :], number(1, full), ALU.add))
                chain(tt(h[:, :, :], h[:, :, :], hpos[:, :, :], ALU.add))
                pool.wait_ge(x_res_landed, 16 * (g + 1))
                tt(h[:, :, :], h[:, :, :], x_res[:, :, :], ALU.add).then_inc(res_ready, 1)
                pool.wait_ge(mv_ready, g + 1)
                chain(tt(veps[:, :], mv[:, :, 1], number(2, few), ALU.add))
                tt(rstd[:, :], veps[:, :], number(3, few), ALU.pow)
                if type(g) is not int or g > 0:
                    pool.wait_ge(out_stored, 16 * g)
                chain(tt(y_out[:, :, :], h[:, :, :], rows(mv[:, :, 0]), ALU.subtract))
                tt(y_out[:, :, :], y_out[:, :, :], rows(rstd[:, :]), ALU.mult).then_inc(y_ready, 1)
                assert n[0] == STEPS, n[0]

            epilogue(0)
            with pool.Fori(1, NG) as g:
                epilogue(g)

        @block.scalar
        def _(act):
            for g in range(NG):
                act.wait_ge(xt_ready, g + 1)
                if g >= 2:
                    act.wait_ge(wh_ready, g - 1)
                nc.scalar.copy(x_t[g % 2][:, :], p_xt[g % 2]).then_inc(xt_copied, 1)
                act.wait_ge(wh_ready, g + 1)
                nc.scalar.copy(s_row[:, g * GROUP:(g + 1) * GROUP], p_srow[g % 2]).then_inc(srow_copied, 1)
            act.wait_ge(z_ready, 1)
            nc.scalar.activation(q1[:, :], neg_t[:, :], ACT.Exp, bias=stat[:, 4:5], scale=-1.0).then_inc(q_ready, 1)
            nc.scalar.activation(q2[:, :], neg_t[:, :], ACT.Exp, bias=stat[:, 5:6], scale=-LEAK).then_inc(q_ready, 1)
            nc.scalar.activation(alpha[:, :], zmin[:, :], ACT.Exp).then_inc(q_ready, 1)
            nc.scalar.activation(beta[:, :], zmax[:, :], ACT.Exp, scale=-1.0).then_inc(q_ready, 1)
            for o in range(NOCT):
                for k in range(2):
                    act.wait_ge(v32_ready, 2 * o + k + 1)
                    nc.scalar.copy(V[:, o * OCT:(o + 1) * OCT, 2 * k, :], v32[k][:, :, :]).then_inc(v_high, 1)

            def edges(n, u, first):
                act.wait_ge(psT_ready, n + 1)
                if not (first and u < EB):
                    act.wait_ge(neg_ready, n - EB + 1)
                nc.scalar.activation(edge[u % EB], psT[u % 2][:, :].bitcast(I32), ACT.Tanh,
                                     bias=edge_bias[:, 0:1], scale=EDGE_GAIN).then_inc(edge_ready, 1)

            def evacuate(g):
                act.wait_ge(unit_used, UNITS * g + UNITS)
                for r in range(RB):
                    nc.scalar.activation(low_part[:, r, :], acc[r][:, C1:2 * C1], ACT.Copy,
                                         scale=beta[:, bass.ds(g * RB + r, 1)]).then_inc(low_ready, 1)

            def elu(g):
                act.wait_ge(h_ready, g + 1)
                nc.scalar.activation(hpos[:, :, :], h[:, :, :], ACT.Relu).then_inc(elu_parts, 1)
                nc.scalar.activation(hneg[:, :, :], h[:, :, :], ACT.Relu, scale=-1.0).then_inc(elu_parts, 1)
                act.wait_ge(elu_parts, 3 * g + 2)
                nc.scalar.activation(hneg[:, :, :], hneg[:, :, :], ACT.Exp, scale=-1.0).then_inc(elu_parts, 1)

            def store(g):
                act.wait_ge(y_ready, g + 1)
                act.dma_start(out_rows[:, bass.ds(g * RB, RB), :], y_out[:, :, :]).then_inc(out_stored, 16)

            def load_res(g):
                if type(g) is not int or g > 0:
                    act.wait_ge(res_ready, g)
                act.dma_start(x_res[:, :, :], x_rows[:, bass.ds(g * RB, RB), :]).then_inc(x_res_landed, 16)

            def group(g, first):
                for u in range(BODY):
                    edges(g * UNITS + u, u, first)
                    if u == 1 and not first:
                        evacuate(g - 1)
                        load_res(g - 1)
                for u in range(BODY):
                    edges(g * UNITS + BODY + u, BODY + u, first)
                if not first:
                    elu(g - 1)
                for u in range(BODY):
                    edges(g * UNITS + 2 * BODY + u, 2 * BODY + u, first)
                if not first:
                    store(g - 1)
                with act.Fori(3, NBODY) as b:
                    for u in range(BODY):
                        edges(g * UNITS + b * BODY + u, u, False)

            group(0, True)
            with act.Fori(1, NG) as g:
                group(g, False)
            evacuate(NG - 1)
            load_res(NG - 1)
            elu(NG - 1)
            store(NG - 1)

        @block.vector
        def _(dve):
            chained = [0]

            def link(ins):
                ins.then_inc(dve_step, 1)
                chained[0] += 1
                dve.wait_ge(dve_step, chained[0])

            dve.wait_ge(wt_ready, 1)
            nc.vector.tensor_copy(w_t[:, :], p_xt[0][:, 0:D]).then_inc(wt_copied, 1)
            dve.wait_ge(wt_ready, 2)
            dve.wait_ge(consts_ready, 3)
            link(nc.vector.tensor_copy(w_in[:, D:D + 1], p_srow[0][:, 1:2]))
            link(nc.vector.tensor_copy(w_in[:, D + 1:CW], p_srow[0][:, 0:1]))
            nc.vector.tensor_scalar(wa1[:, :], ones[:, :], w_in[:, D + 1:CW], None, ALU.mult).then_inc(wt_copied, 1)
            for g in range(NG):
                dve.wait_ge(wh_ready, g + 1)
                for k in range(2):
                    c = g * RB + 2 * k
                    nc.vector.tensor_copy(wh[:, c:c + 2, :],
                                          p_wh[g % 2][k].rearrange("p (c w) -> p c w", w=CW)).then_inc(wh_copied, 1)
                dve.wait_ge(wh_copied, 2 * g + 2)
                link(nc.vector.tensor_reduce(gmax[:, g:g + 1], wh[:, g * RB:(g + 1) * RB, 0:D], AX.XY, ALU.max,
                                             apply_absolute_value=True))
            link(nc.vector.tensor_reduce(stat[:, 1:2], gmax[:, :], AX.X, ALU.max))
            link(nc.vector.tensor_scalar(neg_t[:, :], wh[:, :, D], -1.0, None, ALU.mult))
            nc.vector.tensor_reduce(stat[:, 0:1], wh[:, :, D], AX.X, ALU.max).then_inc(pmax_in, 1)
            dve.wait_ge(pmax_out, 1)
            link(nc.vector.tensor_scalar(stat[:, 4:5], stat[:, 2:3], -1.0, None, ALU.mult))
            link(nc.vector.tensor_scalar(stat[:, 5:6], stat[:, 2:3], -LEAK, None, ALU.mult))
            link(nc.vector.tensor_scalar(z08[:, :], wh[:, :, D + 1], stat[:, 2:3], 1.0 - LEAK, ALU.add, ALU.mult))
            link(nc.vector.tensor_scalar(zmin[:, :], z08[:, :], 0.0, None, ALU.min))
            link(nc.vector.tensor_scalar(wh_max[:, :], stat[:, 3:4], TINY, None, ALU.max))
            nc.vector.tensor_scalar(zmax[:, :], z08[:, :], 0.0, None, ALU.max).then_inc(z_ready, 1)
            link(nc.vector.reciprocal(stat[:, 6:7], wh_max[:, :]))
            link(nc.vector.tensor_scalar(stat[:, 7:8], stat[:, 6:7], V_TOP, None, ALU.mult))
            link(nc.vector.tensor_scalar(stat[:, 8:9], stat[:, 6:7], 1.0 / N, None, ALU.mult))
            link(nc.vector.tensor_scalar(wh[:, :, D], wh[:, :, D], 0.0, wh_max[:, 0:1], ALU.mult, ALU.add))
            dve.wait_ge(wt_ready, 3)
            link(nc.vector.tensor_scalar(mean_wh[:, :], p_xt[0][:, 0:D], stat[:, 8:9], None, ALU.mult))
            dve.wait_ge(q_ready, 2)
            link(nc.vector.tensor_scalar(q1[:, :], q1[:, :], stat[:, 7:8], None, ALU.mult))
            link(nc.vector.tensor_scalar(q2[:, :], q2[:, :], stat[:, 7:8], None, ALU.mult))
            for o in range(NOCT):
                for k, q in enumerate((q1, q2)):
                    for c in range(OCT):
                        ins = nc.vector.tensor_scalar(v32[k][:, c, :], wh[:, o * OCT + c, 0:C1],
                                                      q[:, o * OCT + c:o * OCT + c + 1], None, ALU.mult)
                    ins.then_inc(v32_ready, 1)
                for k in range(2):
                    dve.wait_ge(v_high, 2 * o + k + 1)
                    nc.vector.tensor_tensor(V[:, o * OCT:(o + 1) * OCT, 2 * k + 1, :], v32[k][:, :, :],
                                            V[:, o * OCT:(o + 1) * OCT, 2 * k, :], ALU.subtract).then_inc(v_low, 1)
                dve.wait_ge(v_low, 2 * o + 2)

            dve.wait_ge(srow_copied, NG)

            def split(g, n, c0, u, first):
                dve.wait_ge(edge_ready, n + 1)
                if not (first and u < EB):
                    dve.wait_ge(unit_used, n - EB + 1)
                for c in range(CPU_):
                    nc.vector.scalar_tensor_tensor(
                        pos[u % EB][:, c * GROUP:(c + 1) * GROUP], s_row[:, bass.ds(g * GROUP, GROUP)],
                        neg_t[:, bass.ds(c0 + c, 1)], edge[u % EB][:, c * GROUP:(c + 1) * GROUP],
                        ALU.is_le, ALU.is_lt).then_inc(pos_ready, 1)
                dve.wait_ge(pos_ready, CPU_ * n + CPU_)
                nc.vector.tensor_tensor(neg[u % EB], pos[u % EB], edge[u % EB], ALU.is_lt).then_inc(neg_ready, 1)

            def combine(g):
                for r in range(RB):
                    dve.wait_ge(low_ready, RB * g + r + 1)
                    nc.vector.scalar_tensor_tensor(mix[:, r, :], acc[r][:, 0:C1], alpha[:, bass.ds(g * RB + r, 1)],
                                                   low_part[:, r, :], ALU.mult, ALU.add).then_inc(mix_ready, 1)

            def invert(g):
                dve.wait_ge(mix_ready, RB * g + RB)
                nc.vector.tensor_scalar(empty[:, :], mix[:, :, D], 0.0, None, ALU.is_equal).then_inc(inverse_ready, 1)
                nc.vector.scalar_tensor_tensor(den[:, :], mix[:, :, D], 0.0, mix[:, :, D], ALU.is_equal,
                                               ALU.add).then_inc(den_ready, 1)
                dve.wait_ge(den_ready, g + 1)
                nc.vector.reciprocal(rden[:, :], den[:, :]).then_inc(inverse_ready, 1)

            def statistics(g):
                dve.wait_ge(res_ready, g + 1)
                for r in range(RB):
                    nc.vector.bn_stats(bn[:, r, :], h[:, r, :]).then_inc(bn_done, 1)

            def aggregate():
                for r in range(RB):
                    ins = nc.vector.bn_aggr(mv[:, r, :], bn[:, r, :])
                ins.then_inc(mv_ready, 1)

            def group(g, first):
                for u in range(BODY):
                    split(g, g * UNITS + u, CPU_ * u, u, first)
                    if u == 1 and not first:
                        combine(g - 1)
                    if u == 5 and not first:
                        invert(g - 1)
                for u in range(BODY):
                    split(g, g * UNITS + BODY + u, CPU_ * (BODY + u), BODY + u, first)
                for u in range(BODY):
                    if u == 5 and not first:
                        dve.wait_ge(bn_done, RB * g)
                    split(g, g * UNITS + 2 * BODY + u, CPU_ * (2 * BODY + u), 2 * BODY + u, first)
                    if u == 4 and not first:
                        statistics(g - 1)
                    if u == 5 and not first:
                        aggregate()
                with dve.Fori(3, NBODY) as b:
                    for u in range(BODY):
                        split(g, g * UNITS + b * BODY + u, b * (CPU_ * BODY) + CPU_ * u, u, False)

            group(0, True)
            with dve.Fori(1, NG) as g:
                group(g, False)
            combine(NG - 1)
            invert(NG - 1)
            statistics(NG - 1)
            dve.wait_ge(bn_done, RB * NG)
            aggregate()

        @block.tensor
        def _(pe):
            mm = nc.tensor.matmul
            pe.wait_ge(w_in_landed, 32)
            pe.wait_ge(consts_ready, 3)
            nc.tensor.transpose(p_xt[0][:, 0:D], w_in[:, 0:D], ident[:, :]).then_inc(wt_ready, 1)
            pe.wait_ge(wt_copied, 1)
            mm(p_srow[0][:, 0:2], w_t[:, :], a_in[:, :], start=True, stop=True).then_inc(wt_ready, 1)
            pe.wait_ge(wt_copied, 2)
            for g in range(NG):
                pe.wait_ge(x_landed[g % 2], 16 * (g // 2 + 1))
                if g >= 2:
                    pe.wait_ge(xt_copied, g - 1)
                for r in range(RB):
                    ins = nc.tensor.transpose(p_xt[g % 2][:, r * P:(r + 1) * P], x_nat[g % 2][:, r, :], ident[:, :])
                ins.then_inc(xt_ready, 1)
                pe.wait_ge(xt_copied, g + 1)
                if g >= 2:
                    pe.wait_ge(wh_copied, 2 * (g - 1))
                    pe.wait_ge(srow_copied, g - 1)
                mm(p_srow[g % 2], wa1[:, :], x_t[g % 2][:, :], start=True, stop=True)
                for r in range(RB):
                    ins = mm(p_wh[g % 2][r // 2][:, (r % 2) * CW:(r % 2 + 1) * CW], x_t[g % 2][:, r * P:(r + 1) * P],
                             w_in[:, :], start=True, stop=True)
                ins.then_inc(wh_ready, 1)
            pe.wait_ge(srow_copied, NG)
            pe.wait_ge(xt_copied, NG)
            pe.wait_ge(wh_copied, 2 * NG)
            for c in range(NC):
                ins = mm(p_xt[0][:, 0:D], ones[:, :], wh[:, c, 0:D], start=(c == 0), stop=(c == NC - 1))
            ins.then_inc(wt_ready, 1)
            pe.wait_ge(v_low, 2 * NOCT)

            def transposes(n, j, u, landed):
                if u % SLAB_U == 0:
                    k = (u // SLAB_U) % RING
                    pe.wait_ge(slab_landed[k], landed)
                if not (type(n) is int and n < 2):
                    pe.wait_ge(edge_ready, n - 1)
                k = (u // SLAB_U) % RING
                for c in range(CPU_):
                    cc = (u % SLAB_U) * CPU_ + c
                    for r in range(RB):
                        ins = nc.tensor.transpose(
                            psT[u % 2][:, (c * RB + r) * P:(c * RB + r + 1) * P],
                            slab[k][:, r, cc * P:(cc + 1) * P].bitcast(F32), ident[:, :])
                ins.then_inc(psT_ready, 1)

            def products(n, c0, u, begins, ends, boundary):
                pe.wait_ge(neg_ready, n + 1)
                for c in range(CPU_):
                    for r in range(RB):
                        if begins and c == 0 and boundary is not None:
                            pe.wait_ge(mix_ready, boundary + r)
                        at = (c * RB + r) * P
                        start, stop = begins and c == 0, ends and c == CPU_ - 1
                        for k, m in ((0, pos), (1, pos), (2, neg), (3, neg)):
                            half = acc[r][:, (k // 2) * C1:(k // 2 + 1) * C1]
                            ins = mm(half, m[u % EB][:, at:at + P], V[:, bass.ds(c0 + c, 1), k, :],
                                     start=start and k == 0, stop=stop and k == 3, skip_group_check=True)
                ins.then_inc(unit_used, 1)

            def body(g, b, first):
                for u in range(BODY):
                    n = g * UNITS + b * BODY + u
                    transposes(n, None, u, 16 * (g * NBODY + b + 1))
                    if type(b) is int and b == 0 and u < 2:
                        if not first:
                            products(n - 2, NC - 2 * CPU_ + u * CPU_, (u - 2) % EB, False, u == 1, None)
                        continue
                    begins = type(b) is int and b == 0 and u == 2
                    products(n - 2, b * (CPU_ * BODY) + (u - 2) * CPU_, (u - 2) % EB, begins, False,
                             None if first or not begins else RB * g - RB + 1)

            def group(g, first):
                body(g, 0, first)
                with pe.Fori(1, NBODY) as b:
                    body(g, b, first)

            group(0, True)
            with pe.Fori(1, NG) as g:
                group(g, False)
            products(NG * UNITS - 2, NC - 2 * CPU_, (-2) % EB, False, False, None)
            products(NG * UNITS - 1, NC - CPU_, (-1) % EB, False, True, None)


_INS = ["x", "adj", "L0_gnn_W", "L0_gnn_a"]


def kernel(**inputs):
    import numpy as _np
    import concourse.bacc as _bacc
    from concourse import mybir as _mybir
    from concourse.bass_utils import run_bass_kernel_spmd as _run

    nc = _bacc.Bacc("TRN2", target_bir_lowering=False, num_devices=1)
    arrays, args = {}, []
    for name in _INS:
        a = _np.ascontiguousarray(inputs[name])
        arrays[f"in_{name}_dram"] = a
        args.append(nc.dram_tensor(f"in_{name}_dram", a.shape, _mybir.dt.from_np(a.dtype), kind="ExternalInput").ap())
    shape = inputs["x"].shape
    args.append(nc.dram_tensor("out_0_dram", shape, _mybir.dt.float32, kind="ExternalOutput").ap())
    gat_kernel(nc, *args)
    r = _run(nc, [arrays], core_ids=[0])
    return r.results[0]["out_0_dram"]
```

```python
from contextlib import ExitStack

import concourse.bass as bass
from concourse import mybir

ALU = mybir.AluOpType
ACT = mybir.ActivationFunctionType
F32 = mybir.dt.float32
F16 = mybir.dt.float16
I32 = mybir.dt.int32
AX = mybir.AxisListType
RMAX = bass.bass_isa.ReduceOp.max

P = 128
LEAK = 0.2
LN_EPS = 1e-5
TINY = 1e-30
V_TOP = 16384.0
EDGE_GAIN = 100.0



def gat_kernel(nc, x, adj, W, a, out):
    N, D = x.shape
    assert D == P and N % 512 == 0
    RB = 4
    GROUP = RB * P
    NG = N // GROUP
    NC = N // P
    UC = 2
    UNITS = NC // UC
    SC = 4
    SLABS = NC // SC
    SU = SC // UC
    RING = 4
    UB = 4
    EB = UB // SU
    C1 = D + 1
    CW = D + 2
    SLAB = SC * GROUP

    with ExitStack() as ctx:
        def sb(name, shape, dt):
            return ctx.enter_context(nc.sbuf_tensor(name, shape, dt))

        def ps(name, shape, dt):
            return ctx.enter_context(nc.psum_tensor(name, shape, dt))

        def sem(name):
            return ctx.enter_context(nc.semaphore(name))

        slab = [sb(f"slab{k}", [P, RB, SC * P], I32) for k in range(RING)]
        mask = [sb(f"mask{k}", [P, RB, SC * P], F16) for k in range(2)]
        V = sb("V", [P, NC, 4, C1], F16)
        s_row = sb("s_row", [P, N], F32)
        neg_t = sb("neg_t", [P, NC], F32)
        alpha = sb("alpha", [P, NC], F32)
        beta = sb("beta", [P, NC], F32)
        ident = sb("ident", [P, P], F32)
        edge_bias = sb("edge_bias", [P, 1], F32)
        wh_max = sb("wh_max", [P, 1], F32)
        mean_wh = sb("mean_wh", [P, D], F32)
        shared = sb("shared", [P, NC * CW], F32)
        wh = shared[:, :].rearrange("p (c w) -> p c w", w=CW)
        halves = shared[:, :].bitcast(F16)
        edge = [halves[:, k * SLAB:(k + 1) * SLAB] for k in range(EB)]
        pos_all = halves[:, EB * SLAB:2 * EB * SLAB]
        neg_all = halves[:, 2 * EB * SLAB:3 * EB * SLAB]
        UW = UC * GROUP
        pos = [pos_all[:, k * UW:(k + 1) * UW] for k in range(UB)]
        neg = [neg_all[:, k * UW:(k + 1) * UW] for k in range(UB)]
        w_in = sb("w_in", [P, CW], F32)
        w_t = sb("w_t", [P, D], F32)
        a_in = sb("a_in", [P, 2], F32)
        ones = sb("ones", [P, P], F32)
        wa1 = sb("wa1", [P, P], F32)
        x_nat = [sb(f"x_nat{k}", [P, RB, D], F32) for k in range(2)]
        x_t = [sb(f"x_t{k}", [P, GROUP], F32) for k in range(2)]
        q1 = sb("q1", [P, NC], F32)
        q2 = sb("q2", [P, NC], F32)
        z08 = sb("z08", [P, NC], F32)
        zmin = sb("zmin", [P, NC], F32)
        zmax = sb("zmax", [P, NC], F32)
        stat = sb("stat", [P, 16], F32)
        gmax = sb("gmax", [P, NG], F32)
        ident_h = sb("ident_h", [P, P], F16)
        x_res = sb("x_res", [P, RB, D], F32)
        low_part = sb("low_part", [P, RB, C1], F32)
        mix = sb("mix", [P, RB, C1], F32)
        empty = sb("empty", [P, RB], F32)
        den = sb("den", [P, RB], F32)
        rden = sb("rden", [P, RB], F32)
        rscale = sb("rscale", [P, RB], F32)
        fill = sb("fill", [P, RB, D], F32)
        h = sb("h", [P, RB, D], F32)
        hneg = sb("hneg", [P, RB, D], F32)
        hpos = sb("hpos", [P, RB, D], F32)
        bn = sb("bn", [P, RB, 6], F32)
        mv = sb("mv", [P, RB, 2], F32)
        numbers = sb("numbers", [P, 4], F32)
        veps = sb("veps", [P, RB], F32)
        rstd = sb("rstd", [P, RB], F32)
        y_out = sb("y_out", [P, RB, D], F32)

        psT = [ps(f"psT{k}", [P, SLAB], F16) for k in range(2)]
        acc = [ps(f"acc{r}", [P, 512], F32) for r in range(RB)]
        p_xt = [psT[k][:, 0:2 * GROUP].bitcast(F32) for k in range(2)]
        p_srow = [psT[k][:, 2 * GROUP:4 * GROUP].bitcast(F32) for k in range(2)]
        p_wh = [[acc[2 * k][:, 0:2 * CW], acc[2 * k + 1][:, 0:2 * CW]] for k in range(2)]

        w_in_landed = sem("w_in_landed")
        x_landed = [sem(f"x_landed{k}") for k in range(2)]
        slab_landed = [sem(f"slab_landed{k}") for k in range(RING)]
        x_res_landed = sem("x_res_landed")
        out_stored = sem("out_stored")
        consts_ready = sem("consts_ready")
        wt_ready = sem("wt_ready")
        wt_copied = sem("wt_copied")
        mean_taken = sem("mean_taken")
        xt_ready = sem("xt_ready")
        xt_copied = sem("xt_copied")
        wh_ready = sem("wh_ready")
        wh_copied = sem("wh_copied")
        srow_copied = sem("srow_copied")
        gmax_ready = sem("gmax_ready")
        dve_step = sem("dve_step")
        pmax_in = sem("pmax_in")
        pmax_out = sem("pmax_out")
        z_ready = sem("z_ready")
        q_ready = sem("q_ready")
        qs_ready = sem("qs_ready")
        high1_ready = sem("high1_ready")
        high2_ready = sem("high2_ready")
        low_parts = sem("low_parts")
        mask_ready = sem("mask_ready")
        psT_ready = sem("psT_ready")
        edge_ready = sem("edge_ready")
        pos_ready = sem("pos_ready")
        neg_ready = sem("neg_ready")
        unit_used = sem("unit_used")
        low_ready = sem("low_ready")
        mix_ready = sem("mix_ready")
        den_ready = sem("den_ready")
        inverse_ready = sem("inverse_ready")
        h_ready = sem("h_ready")
        elu_parts = sem("elu_parts")
        res_ready = sem("res_ready")
        bn_done = sem("bn_done")
        mv_ready = sem("mv_ready")
        y_ready = sem("y_ready")
        pool_step = sem("pool_step")

        x_groups = x.rearrange("(g r p) d -> g p r d", r=RB, p=P)
        out_groups = out.rearrange("(g r p) d -> g p r d", r=RB, p=P)
        adj_rows = adj.rearrange("(r p) m -> p r m", p=P)
        x_rows = x.rearrange("(r p) d -> p r d", p=P)
        out_rows = out.rearrange("(r p) d -> p r d", p=P)

        block = ctx.enter_context(nc.Block())

        @block.sync
        def _(sp):
            sp.dma_start(w_in[:, 0:D], W).then_inc(w_in_landed, 16)
            sp.dma_start(a_in[:, :], a.rearrange("(k p) o -> p (k o)", p=P),
                         allow_slow_non_contiguous=True).then_inc(w_in_landed, 16)
            def load_x(g, k, first):
                if not first:
                    sp.wait_ge(xt_ready, g - 1)
                sp.dma_start(x_nat[k][:, :, :], x_rows[:, bass.ds(g * RB, RB), :]).then_inc(x_landed[k], 16)

            for k in range(2):
                load_x(k, k, True)
            with sp.Fori(1, NG // 2) as b:
                for k in range(2):
                    load_x(2 * b + k, k, False)

            def load_slab(g, m, k, first):
                if not first:
                    sp.wait_ge(mask_ready, g * SLABS + m - RING + 1)
                sp.dma_start(slab[k][:, :, :],
                             adj_rows[:, bass.ds(g * RB, RB), bass.ds(m * (SC * P), SC * P)]
                             ).then_inc(slab_landed[k], 16)

            for k in range(RING):
                load_slab(0, k, k, True)
            with sp.Fori(1, SLABS // RING) as b:
                for k in range(RING):
                    load_slab(0, b * RING + k, k, False)
            with sp.Fori(1, NG) as g:
                with sp.Fori(0, SLABS // RING) as b:
                    for k in range(RING):
                        load_slab(g, b * RING + k, k, False)
            sp.wait_ge(out_stored, 16 * NG)

        @block.gpsimd
        def _(pool):
            nc.gpsimd.memset(ones[:, :], 1.0).then_inc(pool_step, 1)
            nc.gpsimd.memset(ident[:, :], 0.0).then_inc(pool_step, 1)
            pool.wait_ge(pool_step, 2)
            nc.gpsimd.affine_select(out=ident[:, :], in_=ident[:, :], compare_op=ALU.not_equal, fill=1.0,
                                    base=0, pattern=[[-1, P]], channel_multiplier=1).then_inc(consts_ready, 1)
            pool.wait_ge(consts_ready, 1)
            nc.gpsimd.tensor_copy(ident_h[:, :], ident[:, :]).then_inc(consts_ready, 1)
            nc.gpsimd.memset(edge_bias[:, :], -EDGE_GAIN / 2).then_inc(consts_ready, 1)
            for k, value in enumerate((0.0, -1.0, LN_EPS, -0.5)):
                ins = nc.gpsimd.memset(numbers[:, k:k + 1], value)
            ins.then_inc(consts_ready, 1)
            pool.wait_ge(pmax_in, 1)
            nc.gpsimd.partition_all_reduce(stat[:, 2:4], stat[:, 0:2], P, RMAX).then_inc(pmax_out, 1)

            pool.wait_ge(qs_ready, 2)
            with pool.Fori(0, NC // SC) as o:
                nc.gpsimd.tensor_tensor(
                    V[:, bass.ds(o * SC, SC), 2, :], wh[:, bass.ds(o * SC, SC), 0:C1],
                    q2[:, bass.ds(o * SC, SC)].unsqueeze(2).broadcast_to([P, SC, C1]), ALU.mult
                    ).then_inc(high2_ready, 1)

            def rows(m):
                return m.unsqueeze(2).broadcast_to([P, RB, D])

            def number(k, shape):
                ap = numbers[:, k:k + 1]
                return ap.unsqueeze(2).broadcast_to(shape) if len(shape) == 3 else ap.broadcast_to(shape)

            tt = nc.gpsimd.tensor_tensor
            full, few = [P, RB, D], [P, RB]
            STEPS = 7

            def epilogue(g):
                base = 2 + g * STEPS
                n = [0]

                def chain(ins):
                    ins.then_inc(pool_step, 1)
                    n[0] += 1
                    pool.wait_ge(pool_step, base + n[0])

                pool.wait_ge(inverse_ready, 2 * g + 2)
                chain(tt(fill[:, :, :], mean_wh[:, :].unsqueeze(1).broadcast_to(full), rows(empty[:, :]), ALU.mult))
                chain(tt(fill[:, :, :], fill[:, :, :], mix[:, :, 0:D], ALU.add))
                chain(tt(rscale[:, :], rden[:, :], wh_max[:, 0:1].broadcast_to(few), ALU.mult))
                tt(h[:, :, :], fill[:, :, :], rows(rscale[:, :]), ALU.mult).then_inc(h_ready, 1)
                pool.wait_ge(elu_parts, 3 * g + 3)
                chain(tt(h[:, :, :], hneg[:, :, :], number(1, full), ALU.add))
                chain(tt(h[:, :, :], h[:, :, :], hpos[:, :, :], ALU.add))
                pool.wait_ge(x_res_landed, 16 * (g + 1))
                tt(h[:, :, :], h[:, :, :], x_res[:, :, :], ALU.add).then_inc(res_ready, 1)
                pool.wait_ge(mv_ready, g + 1)
                chain(tt(veps[:, :], mv[:, :, 1], number(2, few), ALU.add))
                tt(rstd[:, :], veps[:, :], number(3, few), ALU.pow)
                if type(g) is not int or g > 0:
                    pool.wait_ge(out_stored, 16 * g)
                chain(tt(y_out[:, :, :], h[:, :, :], rows(mv[:, :, 0]), ALU.subtract))
                tt(y_out[:, :, :], y_out[:, :, :], rows(rstd[:, :]), ALU.mult).then_inc(y_ready, 1)
                assert n[0] == STEPS, n[0]

            epilogue(0)
            with pool.Fori(1, NG) as g:
                epilogue(g)

        @block.scalar
        def _(act):
            def turn_x(g, k, first):
                act.wait_ge(xt_ready, g + 1)
                if not first:
                    act.wait_ge(wh_ready, g - 1)
                nc.scalar.copy(x_t[k][:, :], p_xt[k]).then_inc(xt_copied, 1)
                if not (type(g) is int and g < 1):
                    keep_s(g - 1, 1 - k)

            def keep_s(g, k):
                act.wait_ge(wh_ready, g + 1)
                nc.scalar.copy(s_row[:, bass.ds(g * GROUP, GROUP)], p_srow[k]).then_inc(srow_copied, 1)

            for k in range(2):
                turn_x(k, k, True)
            with act.Fori(1, NG // 2) as b:
                for k in range(2):
                    turn_x(2 * b + k, k, False)
            keep_s(NG - 1, 1)
            act.wait_ge(z_ready, 1)
            nc.scalar.activation(q1[:, :], neg_t[:, :], ACT.Exp, bias=stat[:, 4:5], scale=-1.0).then_inc(q_ready, 1)
            nc.scalar.activation(q2[:, :], neg_t[:, :], ACT.Exp, bias=stat[:, 5:6], scale=-LEAK).then_inc(q_ready, 1)
            nc.scalar.activation(alpha[:, :], zmin[:, :], ACT.Exp).then_inc(q_ready, 1)
            nc.scalar.activation(beta[:, :], zmax[:, :], ACT.Exp, scale=-1.0).then_inc(q_ready, 1)
            def edges(k, landed, n, first):
                act.wait_ge(slab_landed[k], 16 * landed)
                if not first:
                    act.wait_ge(psT_ready, n - 1)
                nc.scalar.activation(mask[k % 2][:, :, :], slab[k][:, :, :], ACT.Tanh,
                                     bias=edge_bias[:, 0:1], scale=EDGE_GAIN).then_inc(mask_ready, 1)

            for k in range(2):
                edges(k, 1, k, True)
            act.wait_ge(qs_ready, 1)
            with act.Fori(0, NC) as c:
                nc.scalar.activation(V[:, bass.ds(c, 1), 0, :], wh[:, bass.ds(c, 1), 0:C1], ACT.Copy,
                                     scale=q1[:, bass.ds(c, 1)]).then_inc(high1_ready, 1)
            act.wait_ge(low_parts, 2 * NC)

            def turned(n, k, first):
                act.wait_ge(psT_ready, n + 1)
                if not first:
                    act.wait_ge(neg_ready, SU * (n - EB + 1))
                nc.scalar.copy(edge[k % EB], psT[k % 2][:, :]).then_inc(edge_ready, 1)

            def evacuate(g):
                act.wait_ge(unit_used, UNITS * g + UNITS)
                for r in range(RB):
                    nc.scalar.activation(low_part[:, r, :], acc[r][:, C1:2 * C1], ACT.Copy,
                                         scale=beta[:, bass.ds(g * RB + r, 1)]).then_inc(low_ready, 1)

            def elu(g):
                act.wait_ge(h_ready, g + 1)
                nc.scalar.activation(hpos[:, :, :], h[:, :, :], ACT.Relu).then_inc(elu_parts, 1)
                nc.scalar.activation(hneg[:, :, :], h[:, :, :], ACT.Relu, scale=-1.0).then_inc(elu_parts, 1)
                act.wait_ge(elu_parts, 3 * g + 2)
                nc.scalar.activation(hneg[:, :, :], hneg[:, :, :], ACT.Exp, scale=-1.0).then_inc(elu_parts, 1)

            def store(g):
                act.wait_ge(y_ready, g + 1)
                act.dma_start(out_rows[:, bass.ds(g * RB, RB), :], y_out[:, :, :]).then_inc(out_stored, 16)

            def load_res(g):
                if type(g) is not int or g > 0:
                    act.wait_ge(res_ready, g)
                act.dma_start(x_res[:, :, :], x_rows[:, bass.ds(g * RB, RB), :]).then_inc(x_res_landed, 16)

            def group(g, first):
                for m in range(SLABS):
                    n = g * SLABS + m
                    if not (first and m < 2):
                        turned(n - 2, m, first and m < 2 + EB)
                    if m == 3 and not first:
                        evacuate(g - 1)
                    if not (first and m < 2):
                        edges(m % RING, g * (SLABS // RING) + m // RING + 1, n, False)
                    if m == 3 and not first:
                        load_res(g - 1)
                    if m == 7 and not first:
                        elu(g - 1)
                    if m == 14 and not first:
                        store(g - 1)

            group(0, True)
            with act.Fori(1, NG) as g:
                group(g, False)
            for k in range(2):
                turned(NG * SLABS - 2 + k, k, False)
            evacuate(NG - 1)
            load_res(NG - 1)
            elu(NG - 1)
            store(NG - 1)

        @block.vector
        def _(dve):
            chained = [0]

            def link(ins):
                ins.then_inc(dve_step, 1)
                chained[0] += 1
                dve.wait_ge(dve_step, chained[0])

            dve.wait_ge(wt_ready, 1)
            nc.vector.tensor_copy(w_t[:, :], p_xt[0][:, 0:D]).then_inc(wt_copied, 1)
            dve.wait_ge(wt_ready, 2)
            dve.wait_ge(consts_ready, 4)
            link(nc.vector.tensor_copy(w_in[:, D:D + 1], p_srow[0][:, 1:2]))
            link(nc.vector.tensor_copy(w_in[:, D + 1:CW], p_srow[0][:, 0:1]))
            nc.vector.tensor_scalar(wa1[:, :], ones[:, :], w_in[:, D + 1:CW], None, ALU.mult).then_inc(wt_copied, 1)
            def keep_wh(g, k):
                dve.wait_ge(wh_ready, g + 1)
                for i in range(2):
                    nc.vector.tensor_copy(wh[:, bass.ds(g * RB + 2 * i, 2), :],
                                          p_wh[k][i].rearrange("p (c w) -> p c w", w=CW)).then_inc(wh_copied, 1)
                dve.wait_ge(wh_copied, 2 * g + 2)
                nc.vector.tensor_reduce(gmax[:, bass.ds(g, 1)], wh[:, bass.ds(g * RB, RB), 0:D], AX.XY, ALU.max,
                                        apply_absolute_value=True).then_inc(gmax_ready, 1)

            with dve.Fori(0, NG // 2) as b:
                for k in range(2):
                    keep_wh(2 * b + k, k)
            dve.wait_ge(gmax_ready, NG)
            link(nc.vector.tensor_reduce(stat[:, 1:2], gmax[:, :], AX.X, ALU.max))
            link(nc.vector.tensor_scalar(neg_t[:, :], wh[:, :, D], -1.0, None, ALU.mult))
            nc.vector.tensor_reduce(stat[:, 0:1], wh[:, :, D], AX.X, ALU.max).then_inc(pmax_in, 1)
            dve.wait_ge(pmax_out, 1)
            link(nc.vector.tensor_scalar(stat[:, 4:5], stat[:, 2:3], -1.0, None, ALU.mult))
            link(nc.vector.tensor_scalar(stat[:, 5:6], stat[:, 2:3], -LEAK, None, ALU.mult))
            link(nc.vector.tensor_scalar(z08[:, :], wh[:, :, D + 1], stat[:, 2:3], 1.0 - LEAK, ALU.add, ALU.mult))
            link(nc.vector.tensor_scalar(zmin[:, :], z08[:, :], 0.0, None, ALU.min))
            link(nc.vector.tensor_scalar(wh_max[:, :], stat[:, 3:4], TINY, None, ALU.max))
            nc.vector.tensor_scalar(zmax[:, :], z08[:, :], 0.0, None, ALU.max).then_inc(z_ready, 1)
            link(nc.vector.reciprocal(stat[:, 6:7], wh_max[:, :]))
            link(nc.vector.tensor_scalar(stat[:, 7:8], stat[:, 6:7], V_TOP, None, ALU.mult))
            link(nc.vector.tensor_scalar(stat[:, 8:9], stat[:, 6:7], 1.0 / N, None, ALU.mult))
            link(nc.vector.tensor_scalar(wh[:, :, D], wh[:, :, D], 0.0, wh_max[:, 0:1], ALU.mult, ALU.add))
            dve.wait_ge(q_ready, 2)
            nc.vector.tensor_scalar(q1[:, :], q1[:, :], stat[:, 7:8], None, ALU.mult).then_inc(qs_ready, 1)
            nc.vector.tensor_scalar(q2[:, :], q2[:, :], stat[:, 7:8], None, ALU.mult).then_inc(qs_ready, 1)
            dve.wait_ge(qs_ready, 2)

            with dve.Fori(0, NC // SC) as o:
                dve.wait_ge(high2_ready, o + 1)
                for i in range(SC):
                    c = o * SC + i
                    dve.wait_ge(high1_ready, o * SC + i + 1)
                    for k, q in ((0, q1), (2, q2)):
                        nc.vector.scalar_tensor_tensor(
                            V[:, bass.ds(c, 1), k + 1, :], wh[:, bass.ds(c, 1), 0:C1], q[:, bass.ds(c, 1)],
                            V[:, bass.ds(c, 1), k, :], ALU.mult, ALU.subtract).then_inc(low_parts, 1)
            dve.wait_ge(wt_ready, 3)
            nc.vector.tensor_scalar(mean_wh[:, :], p_xt[0][:, 0:D], stat[:, 8:9], None, ALU.mult).then_inc(mean_taken, 1)
            dve.wait_ge(low_parts, 2 * NC)
            dve.wait_ge(srow_copied, NG)

            def split(g, n, c0, u, first):
                if u % SU == 0:
                    dve.wait_ge(edge_ready, (n + SU) // SU if type(n) is int else g[1] + 1)
                if not first:
                    dve.wait_ge(unit_used, n - UB + 1)
                e = edge[u // SU][:, (u % SU) * UW:(u % SU + 1) * UW]
                for c in range(UC):
                    at = slice(c * GROUP, (c + 1) * GROUP)
                    nc.vector.scalar_tensor_tensor(
                        pos[u][:, at], s_row[:, bass.ds(g[0] * GROUP, GROUP)], neg_t[:, bass.ds(c0 + c, 1)],
                        e[:, at], ALU.is_le, ALU.is_lt).then_inc(pos_ready, 1)
                dve.wait_ge(pos_ready, UC * n + UC)
                nc.vector.tensor_tensor(neg[u], pos[u], e, ALU.is_lt).then_inc(neg_ready, 1)

            def combine(g):
                for r in range(RB):
                    dve.wait_ge(low_ready, RB * g + r + 1)
                    nc.vector.scalar_tensor_tensor(mix[:, r, :], acc[r][:, 0:C1], alpha[:, bass.ds(g * RB + r, 1)],
                                                   low_part[:, r, :], ALU.mult, ALU.add).then_inc(mix_ready, 1)

            def invert(g):
                dve.wait_ge(mix_ready, RB * g + RB)
                nc.vector.tensor_scalar(empty[:, :], mix[:, :, D], 0.0, None, ALU.is_equal).then_inc(inverse_ready, 1)
                nc.vector.scalar_tensor_tensor(den[:, :], mix[:, :, D], 0.0, mix[:, :, D], ALU.is_equal,
                                               ALU.add).then_inc(den_ready, 1)
                dve.wait_ge(den_ready, g + 1)
                nc.vector.reciprocal(rden[:, :], den[:, :]).then_inc(inverse_ready, 1)

            def statistics(g):
                dve.wait_ge(res_ready, g + 1)
                for r in range(RB):
                    nc.vector.bn_stats(bn[:, r, :], h[:, r, :]).then_inc(bn_done, 1)

            def aggregate():
                for r in range(RB):
                    ins = nc.vector.bn_aggr(mv[:, r, :], bn[:, r, :])
                ins.then_inc(mv_ready, 1)

            def body(g, b, first, after=None):
                for u in range(UB):
                    split((g, g * SLABS + b * EB + u // SU), g * UNITS + b * UB + u, b * (UC * UB) + UC * u, u, first)
                    if after and u in after:
                        after[u]()

            def group(g, first):
                if first:
                    body(g, 0, True)
                    with dve.Fori(1, UNITS // UB) as b:
                        body(g, b, False)
                    return
                body(g, 0, False, {1: lambda: combine(g - 1), 2: lambda: invert(g - 1)})
                with dve.Fori(1, 4) as b:
                    body(g, b, False)
                body(g, 4, False, {0: lambda: statistics(g - 1), 1: lambda: dve.wait_ge(bn_done, RB * g),
                                   2: aggregate})
                with dve.Fori(5, UNITS // UB) as b:
                    body(g, b, False)

            group(0, True)
            with dve.Fori(1, NG) as g:
                group(g, False)
            combine(NG - 1)
            invert(NG - 1)
            statistics(NG - 1)
            dve.wait_ge(bn_done, RB * NG)
            aggregate()

        @block.tensor
        def _(pe):
            mm = nc.tensor.matmul
            pe.wait_ge(w_in_landed, 32)
            pe.wait_ge(consts_ready, 4)
            nc.tensor.transpose(p_xt[0][:, 0:D], w_in[:, 0:D], ident[:, :]).then_inc(wt_ready, 1)
            pe.wait_ge(wt_copied, 1)
            mm(p_srow[0][:, 0:2], w_t[:, :], a_in[:, :], start=True, stop=True).then_inc(wt_ready, 1)
            pe.wait_ge(wt_copied, 2)

            def turn_x(g, k, first):
                pe.wait_ge(x_landed[k], 16 * (g // 2 + 1) if type(g) is int else 16 * (g[1] + 1))
                g = g if type(g) is int else g[0]
                if not first:
                    pe.wait_ge(xt_copied, g - 1)
                for r in range(RB):
                    ins = nc.tensor.transpose(p_xt[k][:, r * P:(r + 1) * P], x_nat[k][:, r, :], ident[:, :])
                ins.then_inc(xt_ready, 1)

            def project_x(g, k, first):
                pe.wait_ge(xt_copied, g + 1)
                if not first:
                    pe.wait_ge(wh_copied, 2 * (g - 1))
                    pe.wait_ge(srow_copied, g - 1)
                mm(p_srow[k], wa1[:, :], x_t[k][:, :], start=True, stop=True)
                for r in range(RB):
                    ins = mm(p_wh[k][r // 2][:, (r % 2) * CW:(r % 2 + 1) * CW], x_t[k][:, r * P:(r + 1) * P],
                             w_in[:, :], start=True, stop=True)
                ins.then_inc(wh_ready, 1)

            turn_x(0, 0, True)
            turn_x(1, 1, True)
            project_x(0, 0, True)
            project_x(1, 1, True)
            with pe.Fori(1, NG // 2) as b:
                for k in range(2):
                    turn_x((2 * b + k, b), k, False)
                for k in range(2):
                    project_x(2 * b + k, k, False)
            pe.wait_ge(srow_copied, NG)
            pe.wait_ge(xt_copied, NG)
            pe.wait_ge(wh_copied, 2 * NG)
            for c in range(NC):
                ins = mm(p_xt[0][:, 0:D], ones[:, :], wh[:, c, 0:D], start=(c == 0), stop=(c == NC - 1))
            ins.then_inc(wt_ready, 1)

            def transposes(n, k, half, first):
                if half == 0:
                    pe.wait_ge(mask_ready, n + 1)
                    if not first:
                        pe.wait_ge(edge_ready, n - 1)
                for c in range(half * UC, half * UC + UC):
                    for r in range(RB):
                        at = (c * RB + r) * P
                        ins = nc.tensor.transpose(psT[k][:, at:at + P], mask[k][:, r, c * P:(c + 1) * P], ident_h[:, :])
                if half == SU - 1:
                    ins.then_inc(psT_ready, 1)

            def products(n, c0, u, begins, ends, taken):
                pe.wait_ge(neg_ready, n + 1)
                for c in range(UC):
                    for r in range(RB):
                        start, stop = begins and c == 0, ends and c == UC - 1
                        if start and taken is not None:
                            pe.wait_ge(mix_ready, taken + r)
                        at = (c * RB + r) * P
                        for k, m in ((0, pos), (1, pos), (2, neg), (3, neg)):
                            half = acc[r][:, (k // 2) * C1:(k // 2 + 1) * C1]
                            ins = mm(half, m[u][:, at:at + P], V[:, bass.ds(c0 + c, 1), k, :],
                                     start=start and k == 0, stop=stop and k == 3, skip_group_check=True)
                ins.then_inc(unit_used, 1)

            def body(g, b, begins=False, taken=None):
                for k in range(2):
                    for i in range(SU):
                        transposes(g * SLABS + b * 2 + k, k, i, False)
                        u = k * SU + i
                        products(g * UNITS + b * UB + u - UB, b * (UC * UB) - UC * UB + UC * u, u,
                                 begins and u == 0, False, taken)

            def seam(g):
                for k in range(2):
                    for i in range(SU):
                        transposes(g * SLABS + k, k, i, False)
                        u = k * SU + i
                        products(g * UNITS + u - UB, NC - UC * UB + UC * u, u, False, u == UB - 1, None)

            for k in range(2):
                if k == 0:
                    pe.wait_ge(low_parts, 2 * NC)
                    pe.wait_ge(mean_taken, 1)
                for i in range(SU):
                    transposes(k, k, i, True)
            body(0, 1, True, None)
            with pe.Fori(2, SLABS // 2) as b:
                body(0, b)
            with pe.Fori(1, NG) as g:
                seam(g)
                body(g, 1, True, RB * g - RB + 1)
                with pe.Fori(2, SLABS // 2) as b:
                    body(g, b)
            for u in range(UB):
                products(NG * UNITS - UB + u, NC - UC * UB + UC * u, u, False, u == UB - 1, None)


_INS = ["x", "adj", "L0_gnn_W", "L0_gnn_a"]


def kernel(**inputs):
    import numpy as _np
    import concourse.bacc as _bacc
    from concourse import mybir as _mybir
    from concourse.bass_utils import run_bass_kernel_spmd as _run

    nc = _bacc.Bacc("TRN2", target_bir_lowering=False, num_devices=1)
    arrays, args = {}, []
    for name in _INS:
        a = _np.ascontiguousarray(inputs[name])
        arrays[f"in_{name}_dram"] = a
        args.append(nc.dram_tensor(f"in_{name}_dram", a.shape, _mybir.dt.from_np(a.dtype), kind="ExternalInput").ap())
    shape = inputs["x"].shape
    args.append(nc.dram_tensor("out_0_dram", shape, _mybir.dt.float32, kind="ExternalOutput").ap())
    gat_kernel(nc, *args)
    r = _run(nc, [arrays], core_ids=[0])
    return r.results[0]["out_0_dram"]
```

```python
from contextlib import ExitStack

import concourse.bass as bass
from concourse import mybir

ALU = mybir.AluOpType
ACT = mybir.ActivationFunctionType
F32 = mybir.dt.float32
F16 = mybir.dt.float16
I32 = mybir.dt.int32
AX = mybir.AxisListType
RMAX = bass.bass_isa.ReduceOp.max

P = 128
LEAK = 0.2
LN_EPS = 1e-5
TINY = 1e-30
V_TOP = 16384.0
MASKED = -9e15
NARROW = 8.0
EDGE_GAIN = 100.0



def gat_kernel(nc, x, adj, W, a, out):
    N, D = x.shape
    assert D == P and N % 512 == 0
    RB = 4
    GROUP = RB * P
    NG = N // GROUP
    NC = N // P
    UC = 2
    UNITS = NC // UC
    SC = 4
    SLABS = NC // SC
    SU = SC // UC
    RING = 4
    UB = 4
    EB = UB // SU
    C1 = D + 1
    CW = D + 2
    XR = 4
    VQ = NC // SC
    VB = 4
    VD = 2
    SLAB = SC * GROUP

    with ExitStack() as ctx:
        def sb(name, shape, dt):
            return ctx.enter_context(nc.sbuf_tensor(name, shape, dt))

        def ps(name, shape, dt):
            return ctx.enter_context(nc.psum_tensor(name, shape, dt))

        def sem(name):
            return ctx.enter_context(nc.semaphore(name))

        slabs = sb("slabs", [P, RING * SLAB], I32)
        slab = [slabs[:, k * SLAB:(k + 1) * SLAB].rearrange("p (r m) -> p r m", r=RB) for k in range(RING)]
        mask = [sb(f"mask{k}", [P, RB, SC * P], F16) for k in range(2)]
        values = sb("values", [P, NC * 4 * C1], F16)
        V = values[:, :].rearrange("p (c k w) -> p c k w", k=4, w=C1)
        s_row = sb("s_row", [P, N], F32)
        neg_t = sb("neg_t", [P, NC], F32)
        alpha = sb("alpha", [P, NC], F32)
        beta = sb("beta", [P, NC], F32)
        ident = sb("ident", [P, P], F32)
        edge_bias = sb("edge_bias", [P, 1], F32)
        wh_max = sb("wh_max", [P, 1], F32)
        mean_wh = sb("mean_wh", [P, D], F32)
        shared = sb("shared", [P, NC * CW], F32)
        wh = shared[:, :].rearrange("p (c w) -> p c w", w=CW)
        halves = shared[:, :].bitcast(F16)
        pos_all = halves[:, 0:EB * SLAB]
        neg_all = halves[:, EB * SLAB:2 * EB * SLAB]
        UW = UC * GROUP
        pos = [pos_all[:, k * UW:(k + 1) * UW] for k in range(UB)]
        neg = [neg_all[:, k * UW:(k + 1) * UW] for k in range(UB)]
        assert N <= RING * SLAB and 2 * N <= NC * 2 * C1
        adj_row = slabs[:, 0:N]
        cap = adj_row.bitcast(F32)
        v_words = values[:, :].bitcast(F32)
        score = v_words[:, 0:N]
        t_row = v_words[:, N:2 * N]
        leaky = s_row
        spare = sb("spare", [P, 1], F32)
        neg_max = sb("neg_max", [P, 1], F32)
        narrow = sb("narrow", [P, 1], I32)
        w_in = sb("w_in", [P, CW], F32)
        w_t = sb("w_t", [P, D], F32)
        a_in = sb("a_in", [P, 2], F32)
        ones = sb("ones", [P, P], F32)
        s_cols = [sb(f"s_cols{k}", [P, RB], F32) for k in range(2)]
        x_edge = sb("x_edge", [P, XR * GROUP], F32)
        x_nat = [x_edge[:, k * GROUP:(k + 1) * GROUP].rearrange("p (r d) -> p r d", r=RB) for k in range(XR)]
        assert EB * SLAB <= 2 * XR * GROUP
        edge = [x_edge[:, :].bitcast(F16)[:, k * SLAB:(k + 1) * SLAB] for k in range(EB)]
        x_t = [sb(f"x_t{k}", [P, GROUP], F32) for k in range(2)]
        q1 = sb("q1", [P, NC], F32)
        q2 = sb("q2", [P, NC], F32)
        z08 = sb("z08", [P, NC], F32)
        zmin = sb("zmin", [P, NC], F32)
        zmax = sb("zmax", [P, NC], F32)
        stat = sb("stat", [P, 16], F32)
        T_MAX, WH_MAX, T_MIN_NEG, T_NEG, T_NEG_LEAK, WH_INV, TO_TOP, TO_MEAN, RANGE, NARROW_F = (
            slice(k, k + 1) for k in range(3, 13))
        gmax = sb("gmax", [P, NG], F32)
        ident_h = sb("ident_h", [P, P], F16)
        scratch = sb("scratch", [P, VB * 2 * SC * C1], F32)
        v_full = [scratch[:, b * 2 * SC * C1:(b + 1) * 2 * SC * C1].rearrange("p (k c w) -> p k c w", k=2, w=C1)
                  for b in range(VB)]
        assert 2 * RB * C1 + 6 * GROUP <= VB * 2 * SC * C1
        neg_part, mix = (scratch[:, k * RB * C1:(k + 1) * RB * C1].rearrange("p (r w) -> p r w", w=C1)
                         for k in range(2))
        wide = scratch[:, 2 * RB * C1:]
        x_res, fill, h, hneg, hpos, y_out = (
            wide[:, k * GROUP:(k + 1) * GROUP].rearrange("p (r d) -> p r d", d=D) for k in range(6))
        rest_part = sb("rest_part", [P, RB, C1], F32)
        empty = sb("empty", [P, RB], F32)
        den = sb("den", [P, RB], F32)
        rden = sb("rden", [P, RB], F32)
        rscale = sb("rscale", [P, RB], F32)
        bn = sb("bn", [P, RB, 6], F32)
        mv = sb("mv", [P, RB, 2], F32)
        numbers = sb("numbers", [P, 3], F32)
        veps = sb("veps", [P, RB], F32)
        rstd = sb("rstd", [P, RB], F32)

        psT = [ps(f"psT{k}", [P, SLAB], F16) for k in range(2)]
        acc = [ps(f"acc{r}", [P, 512], F32) for r in range(RB)]
        p_xt = [psT[k][:, 0:2 * GROUP].bitcast(F32) for k in range(2)]
        p_srow = [psT[k][:, 2 * GROUP:4 * GROUP].bitcast(F32) for k in range(2)]
        p_wh = [[acc[2 * k][:, 0:2 * CW], acc[2 * k + 1][:, 0:2 * CW]] for k in range(2)]

        w_in_landed = sem("w_in_landed")
        x_landed = [sem(f"x_landed{k}") for k in range(XR)]
        slab_landed = [sem(f"slab_landed{k}") for k in range(RING)]
        x_res_landed = sem("x_res_landed")
        out_stored = sem("out_stored")
        consts_ready = sem("consts_ready")
        wt_ready = sem("wt_ready")
        wt_copied = sem("wt_copied")
        mean_taken = sem("mean_taken")
        xt_ready = sem("xt_ready")
        xt_copied = sem("xt_copied")
        wh_ready = sem("wh_ready")
        wh_dve = sem("wh_dve")
        wh_act = sem("wh_act")
        s_cols_dve = sem("s_cols_dve")
        s_cols_act = sem("s_cols_act")
        srow_ready = sem("srow_ready")
        srow_copied = sem("srow_copied")
        gmax_ready = sem("gmax_ready")
        dve_step = sem("dve_step")
        pmax_in = sem("pmax_in")
        pmax_out = sem("pmax_out")
        bias_ready = sem("bias_ready")
        z_ready = sem("z_ready")
        q_ready = sem("q_ready")
        qs_ready = sem("qs_ready")
        full_dve = sem("full_dve")
        full_pool = sem("full_pool")
        high_ready = sem("high_ready")
        low_parts = sem("low_parts")
        mask_ready = sem("mask_ready")
        psT_ready = sem("psT_ready")
        edge_ready = sem("edge_ready")
        pos_ready = sem("pos_ready")
        neg_ready = sem("neg_ready")
        unit_used = sem("unit_used")
        narrow_ready = sem("narrow_ready")
        ones_col = sem("ones_col")
        row_landed = sem("row_landed")
        score_step = sem("score_step")
        scores_ready = sem("scores_ready")
        probs_ready = sem("probs_ready")
        turn_ready = sem("turn_ready")
        turn_copied = sem("turn_copied")
        sums_ready = sem("sums_ready")
        sums_done = sem("sums_done")
        part_ready = sem("part_ready")
        mix_ready = sem("mix_ready")
        total_ready = sem("total_ready")
        den_ready = sem("den_ready")
        inverse_ready = sem("inverse_ready")
        h_ready = sem("h_ready")
        elu_parts = sem("elu_parts")
        res_ready = sem("res_ready")
        bn_done = sem("bn_done")
        rstd_ready = sem("rstd_ready")
        last_step = sem("last_step")
        mv_ready = sem("mv_ready")
        y_ready = sem("y_ready")
        pool_step = sem("pool_step")

        adj_rows = adj.rearrange("(r p) m -> p r m", p=P)
        x_rows = x.rearrange("(r p) d -> p r d", p=P)
        out_rows = out.rearrange("(r p) d -> p r d", p=P)

        def path_of(eng):
            eng.wait_ge(narrow_ready, 1)
            return eng.value_load(narrow[0:1, 0:1], min_val=0, max_val=1)

        block = ctx.enter_context(nc.Block())

        @block.sync
        def _(sp):
            def load_x(b, k, first):
                if not first:
                    sp.wait_ge(xt_ready, b * XR + k - XR + 1)
                sp.dma_start(x_nat[k], x_rows[:, bass.ds((b * XR + k) * RB, RB), :]).then_inc(x_landed[k], 16)

            for k in range(XR):
                load_x(0, k, True)
            with sp.Fori(1, NG // XR) as b:
                for k in range(XR):
                    load_x(b, k, False)

            def load_slab(g, m, k, first):
                if not first:
                    sp.wait_ge(mask_ready, g * SLABS + m - RING + 1)
                sp.dma_start(slab[k][:, :, :],
                             adj_rows[:, bass.ds(g * RB, RB), bass.ds(m * (SC * P), SC * P)]
                             ).then_inc(slab_landed[k], 16)

            for k in range(RING):
                load_slab(0, k, k, True)
            with sp.If(path_of(sp) == 1):
                with sp.Fori(1, SLABS // RING) as b:
                    for k in range(RING):
                        load_slab(0, b * RING + k, k, False)
                with sp.Fori(1, NG) as g:
                    with sp.Fori(0, SLABS // RING) as b:
                        for k in range(RING):
                            load_slab(g, b * RING + k, k, False)
            with sp.Else():
                for k in range(RING):
                    sp.wait_ge(slab_landed[k], 16)
                sp.wait_ge(mask_ready, RING)
                sp.dma_start(adj_row, adj_rows[:, 0, :]).then_inc(row_landed, 16)
                with sp.Fori(1, NC) as i:
                    sp.wait_ge(scores_ready, i)
                    sp.dma_start(adj_row, adj_rows[:, bass.ds(i, 1), :]).then_inc(row_landed, 16)
            sp.wait_ge(out_stored, 16 * (NG + 1))

        @block.gpsimd
        def _(pool):
            nc.gpsimd.memset(ones[:, :], 1.0).then_inc(pool_step, 1)
            nc.gpsimd.memset(ident[:, :], 0.0).then_inc(pool_step, 1)
            pool.wait_ge(pool_step, 2)
            nc.gpsimd.affine_select(out=ident[:, :], in_=ident[:, :], compare_op=ALU.not_equal, fill=1.0,
                                    base=0, pattern=[[-1, P]], channel_multiplier=1).then_inc(consts_ready, 1)
            pool.wait_ge(consts_ready, 1)
            nc.gpsimd.tensor_copy(ident_h[:, :], ident[:, :]).then_inc(consts_ready, 1)
            nc.gpsimd.memset(edge_bias[:, :], -EDGE_GAIN / 2).then_inc(consts_ready, 1)
            for k, value in enumerate((-1.0, LN_EPS, -0.5)):
                ins = nc.gpsimd.memset(numbers[:, k:k + 1], value)
            ins.then_inc(consts_ready, 1)
            pool.wait_ge(pmax_in, 3)
            nc.gpsimd.partition_all_reduce(stat[:, 3:6], stat[:, 0:3], P, RMAX).then_inc(pmax_out, 1)

            pool.wait_ge(qs_ready, 2)

            def full_values(o, first):
                for i in range(VB):
                    if not first:
                        pool.wait_ge(low_parts, VB * (o - 1) + i + 1)
                        pool.wait_ge(high_ready, VB * (o - 1) + i + 1)
                    cs = bass.ds((o * VB + i) * SC, SC)
                    for k, q in ((1, q2), (0, q1)) if i >= VD else ((1, q2),):
                        nc.gpsimd.tensor_tensor(v_full[i][:, k], wh[:, cs, 0:C1],
                                                q[:, cs].unsqueeze(2).broadcast_to([P, SC, C1]), ALU.mult
                                                ).then_inc(full_pool, 1)

            full_values(0, True)
            with pool.Fori(1, VQ // VB) as o:
                full_values(o, False)

            def rows(m):
                return m.unsqueeze(2).broadcast_to([P, RB, D])

            def number(k, shape):
                ap = numbers[:, k:k + 1]
                return ap.unsqueeze(2).broadcast_to(shape) if len(shape) == 3 else ap.broadcast_to(shape)

            tt = nc.gpsimd.tensor_tensor
            full, few = [P, RB, D], [P, RB]
            STEPS = 7

            def epilogue(g):
                base = 2 + g * STEPS
                n = [0]

                def chain(ins):
                    ins.then_inc(pool_step, 1)
                    n[0] += 1
                    pool.wait_ge(pool_step, base + n[0])

                pool.wait_ge(inverse_ready, 2 * g + 2)
                chain(tt(fill[:, :, :], mean_wh[:, :].unsqueeze(1).broadcast_to(full), rows(empty[:, :]), ALU.mult))
                chain(tt(fill[:, :, :], fill[:, :, :], mix[:, :, 0:D], ALU.add))
                chain(tt(rscale[:, :], rden[:, :], wh_max[:, 0:1].broadcast_to(few), ALU.mult))
                tt(h[:, :, :], fill[:, :, :], rows(rscale[:, :]), ALU.mult).then_inc(h_ready, 1)
                pool.wait_ge(elu_parts, 3 * g + 3)
                chain(tt(h[:, :, :], hneg[:, :, :], number(0, full), ALU.add))
                chain(tt(h[:, :, :], h[:, :, :], hpos[:, :, :], ALU.add))
                pool.wait_ge(x_res_landed, 16 * (g + 1))
                tt(h[:, :, :], h[:, :, :], x_res[:, :, :], ALU.add).then_inc(res_ready, 1)
                pool.wait_ge(mv_ready, g + 1)
                chain(tt(veps[:, :], mv[:, :, 1], number(1, few), ALU.add))
                tt(rstd[:, :], veps[:, :], number(2, few), ALU.pow)
                if type(g) is not int or g > 0:
                    pool.wait_ge(out_stored, 16 * g)
                chain(tt(y_out[:, :, :], h[:, :, :], rows(mv[:, :, 0]), ALU.subtract))
                tt(y_out[:, :, :], y_out[:, :, :], rows(rstd[:, :]), ALU.mult).then_inc(y_ready, 1)
                assert n[0] == STEPS, n[0]

            epilogue(0)
            with pool.Fori(1, NG - 1) as g:
                epilogue(g)
            pool.wait_ge(mv_ready, NG)
            tt(veps[:, :], mv[:, :, 1], number(1, few), ALU.add).then_inc(pool_step, 1)
            pool.wait_ge(pool_step, 2 + (NG - 1) * STEPS + 1)
            tt(rstd[:, :], veps[:, :], number(2, few), ALU.pow).then_inc(rstd_ready, 1)

        @block.scalar
        def _(act):
            act.dma_start(w_in[:, 0:D], W).then_inc(w_in_landed, 16)
            act.dma_start(a_in[:, :], a.rearrange("(k p) o -> p (k o)", p=P),
                          allow_slow_non_contiguous=True).then_inc(w_in_landed, 16)

            def turn_x(g, k):
                act.wait_ge(xt_ready, g + 1)
                if not (type(g) is int and g < 2):
                    act.wait_ge(wh_ready, g - 1)
                nc.scalar.copy(x_t[k][:, :], p_xt[k]).then_inc(xt_copied, 1)

            def keep_wh(g, k):
                act.wait_ge(wh_ready, g + 1)
                if not (type(g) is int and g < 2):
                    act.wait_ge(srow_ready, g - 1)
                half = p_wh[k][1].rearrange("p (c w) -> p c w", w=CW)
                nc.scalar.copy(s_cols[k][:, 2:4], half[:, :, D + 1]).then_inc(s_cols_act, 1)
                nc.scalar.copy(wh[:, bass.ds(g * RB + 2, 2), :], half).then_inc(wh_act, 1)

            def keep_s(g, k):
                act.wait_ge(srow_ready, g + 1)
                nc.scalar.copy(s_row[:, bass.ds(g * GROUP, GROUP)], p_srow[k]).then_inc(srow_copied, 1)

            turn_x(0, 0)
            turn_x(1, 1)
            keep_wh(0, 0)
            for g in range(2, 4):
                turn_x(g, g % 2)
                keep_wh(g - 1, 1 - g % 2)
                keep_s(g - 2, g % 2)
            with act.Fori(2, NG // 2) as b:
                for k in range(2):
                    turn_x(2 * b + k, k)
                    keep_wh(2 * b + k - 1, 1 - k)
                    keep_s(2 * b + k - 2, k)
            keep_wh(NG - 1, 1)
            keep_s(NG - 2, 0)
            keep_s(NG - 1, 1)
            act.wait_ge(bias_ready, 2)
            nc.scalar.activation(q1[:, :], neg_t[:, :], ACT.Exp, bias=stat[:, T_NEG], scale=-1.0).then_inc(q_ready, 1)
            nc.scalar.activation(q2[:, :], neg_t[:, :], ACT.Exp, bias=stat[:, T_NEG_LEAK], scale=-LEAK).then_inc(q_ready, 1)

            def factors():
                act.wait_ge(z_ready, 2)
                nc.scalar.activation(alpha[:, :], zmin[:, :], ACT.Exp).then_inc(q_ready, 1)
                nc.scalar.activation(beta[:, :], zmax[:, :], ACT.Exp, scale=-1.0).then_inc(q_ready, 1)

            def edges(k, landed, n, first):
                act.wait_ge(slab_landed[k], 16 * landed)
                if not first:
                    act.wait_ge(psT_ready, n - 1)
                nc.scalar.activation(mask[k % 2][:, :, :], slab[k][:, :, :], ACT.Tanh,
                                     bias=edge_bias[:, 0:1], scale=EDGE_GAIN).then_inc(mask_ready, 1)

            def high_values(o, some):
                for i in some:
                    act.wait_ge(full_dve, VD * o + min(i + 1, VD))
                    act.wait_ge(full_pool, (2 * VB - VD) * o + i + 1 + max(i + 1 - VD, 0))
                    nc.scalar.copy(V[:, bass.ds((VB * o + i) * SC, SC), 0:4:2, :],
                                   v_full[i].rearrange("p k c w -> p c k w")).then_inc(high_ready, 1)

            def turned(n, k, first):
                act.wait_ge(psT_ready, n + 1)
                if not first:
                    act.wait_ge(neg_ready, SU * (n - EB + 1))
                nc.scalar.copy(edge[k % EB], psT[k % 2][:, :]).then_inc(edge_ready, 1)

            assert VQ // VB == 4 and VB == 4 and EB == 2
            high_values(0, range(4))
            factors()
            high_values(1, (0, 1))
            edges(0, 1, 0, True)
            high_values(1, (2, 3))
            high_values(2, (0, 1))
            edges(1, 1, 1, True)
            high_values(2, (2, 3))
            high_values(3, (0,))
            turned(0, 0, True)
            high_values(3, (1, 2, 3))
            edges(2, 1, 2, False)
            turned(1, 1, True)
            edges(3, 1, 3, False)

            def evacuate(g):
                if type(g) is not int or g > 0:
                    act.wait_ge(total_ready, g)
                for r in range(RB):
                    if r < RB - 1:
                        act.wait_ge(sums_done, (RB - 1) * g + r + 1)
                    else:
                        act.wait_ge(unit_used, UNITS * g + UNITS)
                    for part, k, factor in ((neg_part, 2, beta), (rest_part, 1, alpha)):
                        nc.scalar.activation(part[:, r, :], acc[r][:, k * C1:(k + 1) * C1], ACT.Copy,
                                             scale=factor[:, bass.ds(g * RB + r, 1)]).then_inc(part_ready, 1)

            def elu(g):
                act.wait_ge(h_ready, g + 1)
                nc.scalar.activation(hpos[:, :, :], h[:, :, :], ACT.Relu).then_inc(elu_parts, 1)
                nc.scalar.activation(hneg[:, :, :], h[:, :, :], ACT.Relu, scale=-1.0).then_inc(elu_parts, 1)
                act.wait_ge(elu_parts, 3 * g + 2)
                nc.scalar.activation(hneg[:, :, :], hneg[:, :, :], ACT.Exp, scale=-1.0).then_inc(elu_parts, 1)

            def store(g):
                act.wait_ge(y_ready, g + 1)
                act.dma_start(out_rows[:, bass.ds(g * RB, RB), :], y_out[:, :, :]).then_inc(out_stored, 16)

            def load_res(g):
                if type(g) is not int or g > 0:
                    act.wait_ge(res_ready, g)
                act.dma_start(x_res[:, :, :], x_rows[:, bass.ds(g * RB, RB), :]).then_inc(x_res_landed, 16)

            def group(g, first):
                for m in range(RING if first else 0, SLABS):
                    n = g * SLABS + m
                    turned(n - 2, m, False)
                    if m == 3 and not first:
                        evacuate(g - 1)
                    edges(m % RING, g * (SLABS // RING) + m // RING + 1, n, False)
                    if m == 3 and not first:
                        load_res(g - 1)
                    if m == 7 and not first:
                        elu(g - 1)
                    if m == 14 and not first:
                        store(g - 1)

            def general_rows(i):
                act.wait_ge(scores_ready, i + 1)
                nc.scalar.activation(score, score, ACT.Exp, bias=neg_max[:, 0:1]).then_inc(probs_ready, 1)

            def general_group(g):
                load_res(g)
                for r in range(RB):
                    general_rows(g * RB + r)
                elu(g)
                store(g)

            def last_group(g):
                for r in range(RB):
                    act.wait_ge(last_step, 2 * RB + r + 1)
                    nc.scalar.activation(hneg[:, r, :], hneg[:, r, :], ACT.Exp).then_inc(elu_parts, 1)
                for r in range(0, RB, 2):
                    act.wait_ge(y_ready, g + r + 2)
                    act.dma_start(out_rows[:, g * RB + r:g * RB + r + 2, :], y_out[:, r:r + 2, :]).then_inc(out_stored, 16)

            with act.If(path_of(act) == 1):
                group(0, True)
                with act.Fori(1, NG) as g:
                    group(g, False)
                for k in range(2):
                    turned(NG * SLABS - 2 + k, k, False)
                evacuate(NG - 1)
            with act.Else():
                act.wait_ge(low_parts, VQ)
                general_group(0)
                with act.Fori(1, NG - 1) as g:
                    general_group(g)
                for r in range(RB):
                    general_rows((NG - 1) * RB + r)
            load_res(NG - 1)
            last_group(NG - 1)

        @block.vector
        def _(dve):
            chained = [0]

            def link(ins):
                ins.then_inc(dve_step, 1)
                chained[0] += 1
                dve.wait_ge(dve_step, chained[0])

            dve.wait_ge(wt_ready, 1)
            nc.vector.tensor_copy(w_t[:, :], p_wh[0][0][:, 0:D]).then_inc(wt_copied, 1)
            dve.wait_ge(wt_ready, 2)
            nc.vector.tensor_copy(w_in[:, D:D + 1], p_srow[0][:, 1:2]).then_inc(wt_copied, 1)
            nc.vector.tensor_copy(w_in[:, D + 1:CW], p_srow[0][:, 0:1]).then_inc(wt_copied, 1)

            def keep_wh(g, k):
                dve.wait_ge(wh_ready, g + 1)
                if not (type(g) is int and g < 2):
                    dve.wait_ge(srow_ready, g - 1)
                half = p_wh[k][0].rearrange("p (c w) -> p c w", w=CW)
                nc.vector.tensor_copy(s_cols[k][:, 0:2], half[:, :, D + 1]).then_inc(s_cols_dve, 1)
                nc.vector.tensor_copy(wh[:, bass.ds(g * RB, 2), :], half).then_inc(wh_dve, 1)

            def largest_wh(g):
                dve.wait_ge(wh_dve, g + 1)
                dve.wait_ge(wh_act, g + 1)
                nc.vector.tensor_reduce(gmax[:, bass.ds(g, 1)], wh[:, bass.ds(g * RB, RB), 0:D], AX.XY, ALU.max,
                                        apply_absolute_value=True).then_inc(gmax_ready, 1)

            keep_wh(0, 0)
            keep_wh(1, 1)
            largest_wh(0)
            with dve.Fori(1, NG // 2) as b:
                for k in range(2):
                    keep_wh(2 * b + k, k)
                    largest_wh(2 * b + k - 1)
            largest_wh(NG - 1)
            nc.vector.tensor_reduce(stat[:, 0:1], wh[:, :, D], AX.X, ALU.max).then_inc(pmax_in, 1)
            nc.vector.tensor_reduce(stat[:, 2:3], wh[:, :, D], AX.X, ALU.min, negate=True).then_inc(pmax_in, 1)
            dve.wait_ge(gmax_ready, NG)
            nc.vector.tensor_reduce(stat[:, 1:2], gmax[:, :], AX.X, ALU.max).then_inc(pmax_in, 1)
            link(nc.vector.tensor_scalar(neg_t[:, :], wh[:, :, D], -1.0, None, ALU.mult))
            dve.wait_ge(pmax_out, 1)
            nc.vector.tensor_scalar(stat[:, T_NEG], stat[:, T_MAX], -1.0, None, ALU.mult).then_inc(bias_ready, 1)
            nc.vector.tensor_scalar(stat[:, T_NEG_LEAK], stat[:, T_MAX], -LEAK, None, ALU.mult).then_inc(bias_ready, 1)
            link(nc.vector.tensor_scalar(wh_max[:, :], stat[:, WH_MAX], TINY, None, ALU.max))
            link(nc.vector.reciprocal(stat[:, WH_INV], wh_max[:, :]))
            link(nc.vector.tensor_scalar(stat[:, TO_TOP], stat[:, WH_INV], V_TOP, None, ALU.mult))
            link(nc.vector.tensor_scalar(wh[:, :, D], wh[:, :, D], 0.0, wh_max[:, 0:1], ALU.mult, ALU.add))
            dve.wait_ge(q_ready, 2)
            nc.vector.tensor_scalar(q1[:, :], q1[:, :], stat[:, TO_TOP], None, ALU.mult).then_inc(qs_ready, 1)
            nc.vector.tensor_scalar(q2[:, :], q2[:, :], stat[:, TO_TOP], None, ALU.mult).then_inc(qs_ready, 1)
            dve.wait_ge(qs_ready, 2)

            def full_values(o, i, first):
                if not first:
                    dve.wait_ge(low_parts, VB * (o - 1) + i + 1)
                    dve.wait_ge(high_ready, VB * (o - 1) + i + 1)
                cs = bass.ds((o * VB + i) * SC, SC)
                nc.vector.tensor_tensor(v_full[i][:, 0], wh[:, cs, 0:C1],
                                        q1[:, cs].unsqueeze(2).broadcast_to([P, SC, C1]), ALU.mult
                                        ).then_inc(full_dve, 1)

            def low_values(o, i):
                dve.wait_ge(high_ready, o * VB + i + 1)
                vs = V[:, bass.ds((o * VB + i) * SC, SC)]
                nc.vector.tensor_tensor(vs[:, :, 1:4:2, :], v_full[i].rearrange("p k c w -> p c k w"),
                                        vs[:, :, 0:4:2, :], ALU.subtract).then_inc(low_parts, 1)

            nc.vector.tensor_tensor(stat[:, RANGE], stat[:, T_MAX], stat[:, T_MIN_NEG], ALU.add).then_inc(dve_step, 1)
            nc.vector.tensor_scalar(z08[:, :], wh[:, :, D + 1], stat[:, T_MAX], 1.0 - LEAK, ALU.add,
                                    ALU.mult).then_inc(dve_step, 1)
            chained[0] += 2
            full_values(0, 0, True)
            dve.wait_ge(dve_step, chained[0])
            nc.vector.tensor_scalar(stat[:, NARROW_F], stat[:, RANGE], NARROW, None, ALU.is_le).then_inc(dve_step, 1)
            nc.vector.tensor_scalar(zmin[:, :], z08[:, :], 0.0, None, ALU.min).then_inc(z_ready, 1)
            nc.vector.tensor_scalar(zmax[:, :], z08[:, :], 0.0, None, ALU.max).then_inc(z_ready, 1)
            nc.vector.tensor_scalar(stat[:, TO_MEAN], stat[:, WH_INV], 1.0 / N, None, ALU.mult).then_inc(dve_step, 1)
            chained[0] += 2
            full_values(0, 1, True)
            dve.wait_ge(dve_step, chained[0])
            nc.vector.tensor_copy(narrow[:, :], stat[:, NARROW_F]).then_inc(narrow_ready, 1)
            for i in range(2, VD):
                full_values(0, i, True)
            with dve.Fori(0, VQ // VB - 1) as o:
                for i in range(VB):
                    low_values(o, i)
                    if 1 <= i <= VD:
                        full_values(o + 1, i - 1, False)
            low_values(VQ // VB - 1, 0)
            dve.wait_ge(wt_ready, 3)
            nc.vector.tensor_scalar(mean_wh[:, :], acc[3][:, 0:D], stat[:, TO_MEAN], None, ALU.mult).then_inc(mean_taken, 1)
            path = path_of(dve)
            for i in range(1, VB):
                low_values(VQ // VB - 1, i)
            dve.wait_ge(low_parts, VQ)
            dve.wait_ge(full_pool, VQ // VB * (2 * VB - VD))
            dve.wait_ge(wt_ready, 3)
            dve.wait_ge(srow_copied, NG)

            def split(g, n, c0, u, first):
                if u % SU == 0:
                    dve.wait_ge(edge_ready, (n + SU) // SU if type(n) is int else g[1] + 1)
                if not first:
                    dve.wait_ge(unit_used, n - UB + 1)
                e = edge[u // SU][:, (u % SU) * UW:(u % SU + 1) * UW]
                for c in range(UC):
                    at = slice(c * GROUP, (c + 1) * GROUP)
                    nc.vector.scalar_tensor_tensor(
                        pos[u][:, at], s_row[:, bass.ds(g[0] * GROUP, GROUP)], neg_t[:, bass.ds(c0 + c, 1)],
                        e[:, at], ALU.is_le, ALU.is_lt).then_inc(pos_ready, 1)
                dve.wait_ge(pos_ready, UC * n + UC)
                nc.vector.tensor_tensor(neg[u], pos[u], e, ALU.is_lt).then_inc(neg_ready, 1)

            def combine(g, blocks=range(RB)):
                for r in blocks:
                    dve.wait_ge(part_ready, 2 * (RB * g + r) + 2)
                    nc.vector.scalar_tensor_tensor(mix[:, r, :], acc[r][:, 0:C1], alpha[:, bass.ds(g * RB + r, 1)],
                                                   neg_part[:, r, :], ALU.mult, ALU.add).then_inc(mix_ready, 1)

            def total(g):
                dve.wait_ge(mix_ready, RB * g + RB)
                nc.vector.tensor_tensor(mix[:, :, :], mix[:, :, :], rest_part[:, :, :], ALU.add).then_inc(total_ready, 1)
                dve.wait_ge(total_ready, g + 1)

            def invert(g):
                dve.wait_ge(mix_ready, RB * g + RB)
                nc.vector.tensor_scalar(empty[:, :], mix[:, :, D], 0.0, None, ALU.is_equal).then_inc(inverse_ready, 1)
                nc.vector.scalar_tensor_tensor(den[:, :], mix[:, :, D], 0.0, mix[:, :, D], ALU.is_equal,
                                               ALU.add).then_inc(den_ready, 1)
                dve.wait_ge(den_ready, g + 1)
                nc.vector.reciprocal(rden[:, :], den[:, :]).then_inc(inverse_ready, 1)

            def statistics(g):
                dve.wait_ge(res_ready, g + 1)
                for r in range(RB):
                    nc.vector.bn_stats(bn[:, r, :], h[:, r, :]).then_inc(bn_done, 1)

            def aggregate():
                for r in range(RB):
                    ins = nc.vector.bn_aggr(mv[:, r, :], bn[:, r, :])
                ins.then_inc(mv_ready, 1)

            def body(g, b, first, after=None):
                for u in range(UB):
                    split((g, g * SLABS + b * EB + u // SU), g * UNITS + b * UB + u, b * (UC * UB) + UC * u, u, first)
                    if after and u in after:
                        after[u]()

            def group(g, first):
                if first:
                    body(g, 0, True)
                    with dve.Fori(1, UNITS // UB) as b:
                        body(g, b, False)
                    return
                body(g, 0, False, {1: lambda: combine(g - 1), 2: lambda: total(g - 1),
                                   3: lambda: invert(g - 1)})
                with dve.Fori(1, 4) as b:
                    body(g, b, False)
                body(g, 4, False, {0: lambda: statistics(g - 1), 1: lambda: dve.wait_ge(bn_done, RB * g),
                                   2: aggregate})
                with dve.Fori(5, UNITS // UB) as b:
                    body(g, b, False)

            def general_turns(i, first, out_of):
                with dve.Fori(0, NC // RB) as q:
                    dve.wait_ge(turn_ready, i * (NC // RB) + q + 1)
                    out_of(q).then_inc(turn_copied, 1)

            def general_rows(i):
                step = 3 * i
                dve.wait_ge(row_landed, 16 * (i + 1))
                nc.vector.tensor_scalar(cap, adj_row, 0.0, -0.5, ALU.is_gt, ALU.add)
                nc.vector.tensor_scalar(leaky[:, :], t_row, wh[:, bass.ds(i, 1), D + 1], None,
                                        ALU.add).then_inc(score_step, 1)
                dve.wait_ge(score_step, step + 1)
                nc.vector.scalar_tensor_tensor(leaky[:, :], leaky[:, :], LEAK, leaky[:, :], ALU.mult,
                                               ALU.max).then_inc(score_step, 1)
                dve.wait_ge(score_step, step + 2)
                nc.vector.scalar_tensor_tensor(score, cap, -2.0 * MASKED, leaky[:, :], ALU.mult,
                                               ALU.min).then_inc(score_step, 1)
                dve.wait_ge(score_step, step + 3)
                nc.vector.tensor_reduce(neg_max[:, :], score, AX.X, ALU.max, negate=True).then_inc(scores_ready, 1)
                general_turns(i + 1, False, lambda q: nc.vector.tensor_copy(x_t[0][:, :], p_xt[0]))

            def general_sums(g):
                for r in range(RB):
                    i = g * RB + r
                    general_rows(i)
                    dve.wait_ge(sums_ready, i + 1)
                    nc.vector.tensor_copy(mix[:, r, :], acc[0][:, 0:C1]).then_inc(mix_ready, 1)

            def general_group(g):
                general_sums(g)
                invert(g)
                statistics(g)
                dve.wait_ge(bn_done, RB * g + RB)
                nc.vector.tensor_copy(spare[:, :], neg_max[:, :])
                aggregate()

            def last_group(g):
                invert(g)
                dve.wait_ge(inverse_ready, 2 * g + 2)
                link(nc.vector.tensor_scalar(rscale[:, :], rden[:, :], wh_max[:, 0:1], None, ALU.mult))
                dve.wait_ge(res_ready, g)
                for r in range(RB):
                    nc.vector.scalar_tensor_tensor(fill[:, r, :], mean_wh[:, :], empty[:, r:r + 1], mix[:, r, 0:D],
                                                   ALU.mult, ALU.add).then_inc(last_step, 1)
                for r in range(RB):
                    dve.wait_ge(last_step, r + 1)
                    dve.wait_ge(y_ready, g)
                    nc.vector.tensor_scalar(h[:, r, :], fill[:, r, :], rscale[:, r:r + 1], None,
                                            ALU.mult).then_inc(last_step, 1)
                for r in range(RB):
                    dve.wait_ge(last_step, RB + r + 1)
                    nc.vector.tensor_scalar(hneg[:, r, :], h[:, r, :], 0.0, None, ALU.min).then_inc(last_step, 1)
                for r in range(RB):
                    dve.wait_ge(elu_parts, 3 * g + r + 1)
                    nc.vector.scalar_tensor_tensor(hpos[:, r, :], hneg[:, r, :], -1.0, h[:, r, :],
                                                   ALU.add, ALU.max).then_inc(last_step, 1)
                dve.wait_ge(x_res_landed, 16 * (g + 1))
                for r in range(RB):
                    dve.wait_ge(last_step, 3 * RB + r + 1)
                    nc.vector.tensor_tensor(h[:, r, :], hpos[:, r, :], x_res[:, r, :], ALU.add).then_inc(last_step, 1)
                for r in range(RB):
                    dve.wait_ge(last_step, 4 * RB + r + 1)
                    nc.vector.bn_stats(bn[:, r, :], h[:, r, :]).then_inc(bn_done, 1)
                dve.wait_ge(bn_done, RB * g + RB)
                aggregate()
                dve.wait_ge(rstd_ready, 1)
                dve.wait_ge(out_stored, 16 * g)
                for r in range(RB):
                    nc.vector.tensor_scalar(y_out[:, r, :], h[:, r, :], mv[:, r, 0:1], rstd[:, r:r + 1],
                                            ALU.subtract, ALU.mult).then_inc(y_ready, 1)

            with dve.If(path == 1):
                group(0, True)
                with dve.Fori(1, NG) as g:
                    group(g, False)
                combine(NG - 1)
                total(NG - 1)
            with dve.Else():
                nc.vector.memset(wh[:, :, D], 1.0).then_inc(ones_col, 1)
                nc.vector.memset(wh_max[:, :], 1.0).then_inc(ones_col, 1)
                general_turns(0, True, lambda q: nc.vector.tensor_scalar(
                    t_row[:, bass.ds(q * GROUP, GROUP)], p_xt[0], -1.0, None, ALU.mult))
                dve.wait_ge(turn_copied, NC // RB)
                general_group(0)
                with dve.Fori(1, NG - 1) as g:
                    general_group(g)
                general_sums(NG - 1)
            last_group(NG - 1)

        @block.tensor
        def _(pe):
            mm = nc.tensor.matmul
            pe.wait_ge(w_in_landed, 32)
            pe.wait_ge(consts_ready, 4)
            def turn_x(b, i):
                g, k = b * XR + i, i % 2
                pe.wait_ge(x_landed[i], 16 * (b + 1))
                if not (type(g) is int and g < 2):
                    pe.wait_ge(xt_copied, g - 1)
                for r in range(RB):
                    ins = nc.tensor.transpose(p_xt[k][:, r * P:(r + 1) * P], x_nat[i][:, r, :], ident[:, :])
                ins.then_inc(xt_ready, 1)

            def project_x(g, k):
                pe.wait_ge(xt_copied, g + 1)
                if not (type(g) is int and g < 2):
                    pe.wait_ge(wh_dve, g - 1)
                    pe.wait_ge(wh_act, g - 1)
                    pe.wait_ge(s_cols_dve, g - 1)
                    pe.wait_ge(s_cols_act, g - 1)
                for r in range(RB):
                    ins = mm(p_wh[k][r // 2][:, (r % 2) * CW:(r % 2 + 1) * CW], x_t[k][:, r * P:(r + 1) * P],
                             w_in[:, :], start=True, stop=True)
                ins.then_inc(wh_ready, 1)

            def turn_s(g, k):
                pe.wait_ge(s_cols_dve, g + 1)
                pe.wait_ge(s_cols_act, g + 1)
                if not (type(g) is int and g < 2):
                    pe.wait_ge(srow_copied, g - 1)
                for r in range(RB):
                    ins = nc.tensor.transpose(p_srow[k][:, r * P:(r + 1) * P],
                                              s_cols[k][:, r:r + 1].broadcast_to([P, P]), ident[:, :])
                ins.then_inc(srow_ready, 1)

            nc.tensor.transpose(p_wh[0][0][:, 0:D], w_in[:, 0:D], ident[:, :]).then_inc(wt_ready, 1)
            turn_x(0, 0)
            pe.wait_ge(wt_copied, 1)
            mm(p_srow[0][:, 0:2], w_t[:, :], a_in[:, :], start=True, stop=True).then_inc(wt_ready, 1)
            turn_x(0, 1)
            pe.wait_ge(wt_copied, 3)
            project_x(0, 0)
            for i in range(2, XR):
                turn_x(0, i)
                project_x(i - 1, (i - 1) % 2)
                turn_s(i - 2, i % 2)
            with pe.Fori(1, NG // XR) as b:
                for i in range(XR):
                    turn_x(b, i)
                    project_x(b * XR + i - 1, (i - 1) % 2)
                    turn_s(b * XR + i - 2, i % 2)
            project_x(NG - 1, 1)
            turn_s(NG - 2, 0)
            turn_s(NG - 1, 1)

            pe.wait_ge(wh_dve, NG)
            pe.wait_ge(wh_act, NG)
            for c in range(NC):
                ins = mm(acc[3][:, 0:D], ones[:, :], wh[:, c, 0:D], start=(c == 0), stop=(c == NC - 1))
            ins.then_inc(wt_ready, 1)
            pe.wait_ge(srow_copied, NG)
            pe.wait_ge(xt_copied, NG)

            def transposes(n, k, half, first):
                if half == 0:
                    pe.wait_ge(mask_ready, n + 1)
                    if not first:
                        pe.wait_ge(edge_ready, n - 1)
                for c in range(half * UC, half * UC + UC):
                    for r in range(RB):
                        at = (c * RB + r) * P
                        ins = nc.tensor.transpose(psT[k][:, at:at + P], mask[k][:, r, c * P:(c + 1) * P], ident_h[:, :])
                if half == SU - 1:
                    ins.then_inc(psT_ready, 1)

            def products(n, c0, u, begins, ends, taken):
                pe.wait_ge(neg_ready, n + 1)
                by_chunk = [(c, r) for c in range(UC) for r in range(RB)]
                by_block = [(c, r) for r in range(RB) for c in range(UC)]
                for c, r in by_block if begins or ends else by_chunk:
                    start, stop = begins and c == 0, ends and c == UC - 1
                    if start and taken is not None:
                        pe.wait_ge(mix_ready, taken + r)
                    at = (c * RB + r) * P
                    mask_of, values_of = (pos[u][:, at:at + P], neg[u][:, at:at + P]), V[:, bass.ds(c0 + c, 1)]
                    mm(acc[r][:, 0:2 * C1], mask_of[0], values_of[:, :, 0:2, :], start=start, stop=False,
                       skip_group_check=True)
                    for k in (2, 3):
                        ins = mm(acc[r][:, 2 * C1:3 * C1], mask_of[1], values_of[:, :, k, :], start=False,
                                 stop=stop and k == 3, skip_group_check=True)
                    if stop and r < RB - 1:
                        ins.then_inc(sums_done, 1)
                ins.then_inc(unit_used, 1)

            def body(g, b, begins=False, taken=None):
                for k in range(2):
                    for i in range(SU):
                        if not (begins and k == 0):
                            transposes(g * SLABS + b * 2 + k, k, i, False)
                        elif i == 0:
                            for j in range(SU):
                                transposes(g * SLABS + b * 2, 0, j, False)
                        u = k * SU + i
                        products(g * UNITS + b * UB + u - UB, b * (UC * UB) - UC * UB + UC * u, u,
                                 begins and u == 0, False, taken)

            def seam(g):
                for i in range(SU):
                    transposes(g * SLABS, 0, i, False)
                    products(g * UNITS + i - UB, NC - UC * UB + UC * i, i, False, False, None)
                for i in range(SU):
                    transposes(g * SLABS + 1, 1, i, False)
                for u in range(SU, UB):
                    products(g * UNITS + u - UB, NC - UC * UB + UC * u, u, False, u == UB - 1, None)

            QUADS = NC // RB

            def general_t():
                for q in range(QUADS):
                    if q:
                        pe.wait_ge(turn_copied, q)
                    for k in range(RB):
                        c = q * RB + k
                        ins = nc.tensor.transpose(p_xt[0][:, k * P:(k + 1) * P],
                                                  neg_t[:, c:c + 1].broadcast_to([P, P]), ident[:, :])
                    ins.then_inc(turn_ready, 1)

            def general_rows(i):
                pe.wait_ge(probs_ready, i + 1)
                for q in range(QUADS):
                    pe.wait_ge(turn_copied, (i + 1) * QUADS + q)
                    for k in range(RB):
                        c = q * RB + k
                        ins = nc.tensor.transpose(p_xt[0][:, k * P:(k + 1) * P], score[:, c * P:(c + 1) * P],
                                                  ident[:, :])
                    ins.then_inc(turn_ready, 1)
                    pe.wait_ge(turn_copied, (i + 1) * QUADS + q + 1)
                    if q == 0 and not (type(i) is int and i == 0):
                        pe.wait_ge(mix_ready, i)
                    for k in range(RB):
                        c = q * RB + k
                        ins = mm(acc[0][:, 0:C1], x_t[0][:, k * P:(k + 1) * P], wh[:, c, 0:C1],
                                 start=(c == 0), stop=(c == NC - 1))
                ins.then_inc(sums_ready, 1)

            for k in range(2):
                for i in range(SU):
                    transposes(k, k, i, True)
            path = path_of(pe)
            pe.wait_ge(low_parts, VQ)
            pe.wait_ge(high_ready, VQ)
            pe.wait_ge(mean_taken, 1)
            with pe.If(path == 1):
                body(0, 1, True, None)
                with pe.Fori(2, SLABS // 2) as b:
                    body(0, b)
                with pe.Fori(1, NG) as g:
                    seam(g)
                    body(g, 1, True, RB * g - RB + 1)
                    with pe.Fori(2, SLABS // 2) as b:
                        body(g, b)
                for u in range(UB):
                    products(NG * UNITS - UB + u, NC - UC * UB + UC * u, u, False, u == UB - 1, None)
            with pe.Else():
                pe.wait_ge(ones_col, 2)
                pe.wait_ge(edge_ready, 2)
                general_t()
                general_rows(0)
                with pe.Fori(1, NC) as i:
                    general_rows(i)


_INS = ["x", "adj", "L0_gnn_W", "L0_gnn_a"]


def kernel(**inputs):
    import numpy as _np
    import concourse.bacc as _bacc
    from concourse import mybir as _mybir
    from concourse.bass_utils import run_bass_kernel_spmd as _run

    nc = _bacc.Bacc("TRN2", target_bir_lowering=False, num_devices=1)
    arrays, args = {}, []
    for name in _INS:
        a = _np.ascontiguousarray(inputs[name])
        arrays[f"in_{name}_dram"] = a
        args.append(nc.dram_tensor(f"in_{name}_dram", a.shape, _mybir.dt.from_np(a.dtype), kind="ExternalInput").ap())
    shape = inputs["x"].shape
    args.append(nc.dram_tensor("out_0_dram", shape, _mybir.dt.float32, kind="ExternalOutput").ap())
    gat_kernel(nc, *args)
    r = _run(nc, [arrays], core_ids=[0])
    return r.results[0]["out_0_dram"]
```
